# Optimizing a Trainium2 kernel written in Bass

```python
import numpy as np
import jax
import jax.numpy as jnp

def _softmax(x, axis=-1):
    return jax.nn.softmax(x, axis=axis)

def _gelu(x):
    return jax.nn.gelu(x, approximate=True)

def _silu(x):
    return jax.nn.silu(x)

def _sigmoid(x):
    return jax.nn.sigmoid(x)

def _layernorm(x, axis=-1, eps=1e-05):
    m = jnp.mean(x, axis=axis, keepdims=True)
    v = jnp.var(x, axis=axis, keepdims=True)
    return (x - m) / jnp.sqrt(v + eps)

def _scatter_add(tgt, idx, src, axis=0):
    return tgt.at[idx].add(src)

def _segment_sum(src, seg, n):
    return jax.ops.segment_sum(src, seg, n)
kernel_name = 'mk_cond_resid_d2_seqx_r4_9b525d'

def setup_inputs(seed: int=0):
    np.random.seed(seed)
    _w = jnp.asarray

    def _rec_inputs():
        import jax
        import jax.numpy as jnp
        _rk = jax.random.key(seed)
        x = -0.000125 + 0.9999 * jax.random.normal(jax.random.fold_in(_rk, 1), (8, 256, 256), jnp.float32)
        _lenS = 256 - jax.random.randint(jax.random.fold_in(_rk, 7), (8,), 0, max(1, 256 // 4) + 1, jnp.int32)
        _lenS2 = 256 - jax.random.randint(jax.random.fold_in(_rk, 8), (8,), 0, max(1, 256 // 4) + 1, jnp.int32)
        cond_1024 = -0.00493535 + 1.00056 * jax.random.normal(jax.random.fold_in(_rk, 11), (8, 256), jnp.float32)
        return (x, cond_1024)
    x, cond_1024 = _rec_inputs()

    def _L0_cond_setup():
        import jax, jax.numpy as jnp
        import numpy as np

        def _lstm(x, h0, Wx, Wh, b):
            H = h0.shape[1]
            xW = jnp.einsum('ntd,dk->ntk', x, Wx) + b
            c0 = jnp.zeros_like(h0)

            def step(carry, xw_t):
                prev_h, prev_c = carry
                a = xw_t + prev_h @ Wh
                i = jax.nn.sigmoid(a[:, :H])
                f = jax.nn.sigmoid(a[:, H:2 * H])
                o = jax.nn.sigmoid(a[:, 2 * H:3 * H])
                g = jnp.tanh(a[:, 3 * H:])
                next_c = f * prev_c + i * g
                next_h = o * jnp.tanh(next_c)
                return ((next_h, next_c), next_h)
            _, hs = jax.lax.scan(step, (h0, c0), jnp.swapaxes(xW, 0, 1))
            return jnp.swapaxes(hs, 0, 1)
        key = jax.random.key(seed)
        k_x, k_h0, k_wx, k_wh = jax.random.split(key, 4)
        N, T, D, H = (64, 128, 256, 256)
        x = jax.random.normal(k_x, (N, T, D), dtype=jnp.float32)
        h0 = jax.random.normal(k_h0, (N, H), dtype=jnp.float32)
        Wx = jax.random.normal(k_wx, (D, 4 * H), dtype=jnp.float32) / jnp.sqrt(jnp.float32(D))
        Wh = jax.random.normal(k_wh, (H, 4 * H), dtype=jnp.float32) / jnp.sqrt(jnp.float32(H))
        b = jnp.zeros((4 * H,), dtype=jnp.float32)
        return {'x': x, 'h0': h0, 'Wx': Wx, 'Wh': Wh, 'b': b}
    _L0_cond_all = _L0_cond_setup()
    _L0_cond_in = {k: v for k, v in _L0_cond_all.items() if k in ('Wx', 'Wh', 'b')}
    del _L0_cond_all

    def _L1_cond_setup():
        import jax, jax.numpy as jnp
        import numpy as np
        IN_FEATURES = 256
        OUT_FEATURES = 256
        BATCH = 32
        SEQ = 256
        EPS = 1e-08
        key = jax.random.key(seed)
        k1, k2, k3 = jax.random.split(key, 3)
        Efou = jax.random.normal(k1, (BATCH, SEQ, IN_FEATURES), dtype=jnp.float32)
        y = jax.random.normal(k2, (BATCH, IN_FEATURES), dtype=jnp.float32)
        weight = jax.random.normal(k3, (IN_FEATURES, OUT_FEATURES), dtype=jnp.float32)
        return {'Efou': Efou, 'y': y, 'weight': weight}
    _L1_cond_all = _L1_cond_setup()
    _L1_cond_in = {k: v for k, v in _L1_cond_all.items() if k in ('weight',)}
    del _L1_cond_all
    return {'x': x, 'cond_1024': cond_1024, 'L0_cond_Wx': _L0_cond_in['Wx'], 'L0_cond_Wh': _L0_cond_in['Wh'], 'L0_cond_b': _L0_cond_in['b'], 'L1_cond_weight': _L1_cond_in['weight']}

def reference(x, cond_1024, L0_cond_Wx, L0_cond_Wh, L0_cond_b, L1_cond_weight):
    import jax
    import jax.numpy as jnp

    def _L0_cond_ref(x, h0, Wx, Wh, b):
        import jax, jax.numpy as jnp
        import numpy as np

        def _lstm(x, h0, Wx, Wh, b):
            H = h0.shape[1]
            xW = jnp.einsum('ntd,dk->ntk', x, Wx) + b
            c0 = jnp.zeros_like(h0)

            def step(carry, xw_t):
                prev_h, prev_c = carry
                a = xw_t + prev_h @ Wh
                i = jax.nn.sigmoid(a[:, :H])
                f = jax.nn.sigmoid(a[:, H:2 * H])
                o = jax.nn.sigmoid(a[:, 2 * H:3 * H])
                g = jnp.tanh(a[:, 3 * H:])
                next_c = f * prev_c + i * g
                next_h = o * jnp.tanh(next_c)
                return ((next_h, next_c), next_h)
            _, hs = jax.lax.scan(step, (h0, c0), jnp.swapaxes(xW, 0, 1))
            return jnp.swapaxes(hs, 0, 1)
        return _lstm(x, h0, Wx, Wh, b)

    def _L1_cond_ref(Efou, y, weight):
        import jax, jax.numpy as jnp
        import numpy as np
        IN_FEATURES = 256
        OUT_FEATURES = 256
        BATCH = 32
        SEQ = 256
        EPS = 1e-08
        scale = 1.0 / np.sqrt(np.float32(weight.shape[0]))
        ys = y * scale
        d = jax.lax.rsqrt(jnp.einsum('bi,io->bo', ys * ys, weight * weight) + EPS)
        out = jnp.einsum('bsi,io->bso', Efou * ys[:, None, :], weight) * d[:, None, :]
        return out
    x = x + _L0_cond_ref(x, cond_1024, L0_cond_Wx, L0_cond_Wh, L0_cond_b)
    x = x + _L1_cond_ref(x, cond_1024, L1_cond_weight)
    return x

_drawn_inputs = setup_inputs


def setup_inputs(seed=0):
    import zlib

    import numpy as np

    out = dict(_drawn_inputs(seed))
    spreads = {'L0_cond_b': (0.0, 0.1)}
    factors = {}
    for name, (base, spread) in spreads.items():
        noise = np.random.default_rng([zlib.crc32(name.encode()), seed]).standard_normal(out[name].shape)
        drawn = base * np.exp(spread * noise) if base else spread * noise
        out[name] = jnp.asarray(drawn.astype(out[name].dtype))
    for name, factor in factors.items():
        out[name] = (out[name] * factor).astype(out[name].dtype)
    return out
```

```python
import concourse.bass as bass
from concourse import mybir
from contextlib import ExitStack

F32 = mybir.dt.float32
F16 = mybir.dt.float16
BF16 = mybir.dt.bfloat16
I32 = mybir.dt.int32
ALU = mybir.AluOpType
ACT = mybir.ActivationFunctionType
AX = mybir.AxisListType

P = 128
BT = 16
GATES = 4
EPS = 1e-8


def lstm_modulated_residual(
    nc: bass.Bass,
    x: bass.AP,
    cond: bass.AP,
    Wx: bass.AP,
    Wh: bass.AP,
    b: bass.AP,
    W1: bass.AP,
    out: bass.AP,
):
    N, T, D = x.shape
    HID = D
    KC = D // P
    NB = T // BT
    G4 = GATES * HID
    assert N * BT == P and D == 2 * P and NB % 2 == 0 and NB >= 6
    HALVES = range(KC)

    ctx = ExitStack()
    with ctx:
        def sb(name, shape, dt=F32):
            return ctx.enter_context(nc.sbuf_tensor(name, shape, dt))

        def pb(name, shape, dt=F32):
            return ctx.enter_context(nc.psum_tensor(name, shape, dt))

        def sem(name):
            return ctx.enter_context(nc.semaphore(name))

        wx_sb = sb("wx_sb", [P, KC, G4])
        wh_sb = sb("wh_sb", [P, KC, G4])
        wh_hi = sb("wh_hi", [P, KC, G4], F16)
        wh_lo = sb("wh_lo", [P, KC, G4], F16)
        w1_sb = sb("w1_sb", [P, KC, D])
        w1_sq = sb("w1_sq", [P, KC, D])
        bias_row = sb("bias_row", [1, G4])
        bias_scaled = sb("bias_scaled", [1, G4])
        ones_row = sb("ones_row", [1, P])
        ident = sb("ident", [P, P])
        row_max = sb("row_max", [P, 1])
        all_max = sb("all_max", [P, 1])
        all_max_c = sb("all_max_c", [P, 1])
        max_pow2 = sb("max_pow2", [P, 1])
        inv_pow2 = sb("inv_pow2", [P, 1])
        scale_ifo = sb("scale_ifo", [P, 1])
        scale_g = sb("scale_g", [P, 1])
        scale_b = sb("scale_b", [P, 1])
        unscale = sb("unscale", [P, 1])
        cond_sb = sb("cond_sb", [N, D])
        h0T = sb("h0T", [P, KC, N])
        ys = sb("ys", [P, KC, N])
        ys_sq = sb("ys_sq", [P, KC, N])
        ys_rep = sb("ys_rep", [P, KC, BT, N])
        ys_sq_rep = sb("ys_sq_rep", [P, KC, BT, N])
        demod = sb("demod", [P, D])
        dm_v = sb("dm_v", [P, D])
        dm_root = sb("dm_root", [P, D])
        dm_a = sb("dm_a", [P, D])
        dm_b = sb("dm_b", [P, D])
        x_in = sb("x_in", [P, 2, D])
        XT = sb("XT", [P, 2, KC, BT, N])
        H_all = sb("H_all", [P, 2, KC, BT, N])
        R = sb("R", [P, KC, P])
        Z = sb("Z", [P, KC, P])
        y_sb = sb("y_sb", [P, D])
        r_sb = sb("r_sb", [P, D])
        yd_sb = sb("yd_sb", [P, D])
        o_sb = sb("o_sb", [P, 2, D])
        tg = [[sb(f"tg{q}{h}", [P, GATES + 1, N]) for h in HALVES] for q in range(2)]
        uv = [[sb(f"uv{q}{h}", [P, 2, N]) for h in HALVES] for q in range(2)]
        tc = [[sb(f"tc{q}{h}", [P, N]) for h in HALVES] for q in range(2)]
        H_hi = [[sb(f"H_hi{q}{h}", [P, N], F16) for h in HALVES] for q in range(2)]
        H_lo = [[sb(f"H_lo{q}{h}", [P, N], F16) for h in HALVES] for q in range(2)]

        gate_ps = [[pb(f"gate_ps{q}{h}", [P, GATES, BT, N]) for h in HALVES] for q in range(2)]
        xT_ps = pb("xT_ps", [P, 512])
        y_ps = pb("y_ps", [P, 512])
        r_ps = pb("r_ps", [P, 512])

        x_loaded = [sem(f"x_loaded{q}") for q in range(2)]
        wx_loaded = sem("wx_loaded")
        wh_loaded = sem("wh_loaded")
        b_loaded = sem("b_loaded")
        w1_loaded = sem("w1_loaded")
        cond_loaded = sem("cond_loaded")
        out_stored = [sem(f"out_stored{q}") for q in range(2)]
        ones_set = sem("ones_set")
        ident_zero = sem("ident_zero")
        ident_ready = sem("ident_ready")
        prep = sem("prep")
        max_ready = sem("max_ready")
        allmax_ready = sem("allmax_ready")
        unscale_ready = sem("unscale_ready")
        condT_ready = sem("condT_ready")
        h0_ready = sem("h0_ready")
        wx_scaled = sem("wx_scaled")
        bias_ready = sem("bias_ready")
        wh_scaled = sem("wh_scaled")
        hi_ready = sem("hi_ready")
        split_ready = sem("split_ready")
        c0_ready = sem("c0_ready")
        ysq_ready = sem("ysq_ready")
        norm_ready = sem("norm_ready")
        root_ready = sem("root_ready")
        demod_ready = sem("demod_ready")
        norm_in = sem("norm_in")
        norm_sums = sem("norm_sums")
        gates_ready = [sem(f"gates_ready{h}") for h in HALVES]
        tg_ready = [sem(f"tg_ready{h}") for h in HALVES]
        uv_ready = [sem(f"uv_ready{h}") for h in HALVES]
        c_ready = [sem(f"c_ready{h}") for h in HALVES]
        tc_ready = [sem(f"tc_ready{h}") for h in HALVES]
        hi_made = [sem(f"hi_made{h}") for h in HALVES]
        full_made = [sem(f"full_made{h}") for h in HALVES]
        lo_made = [sem(f"lo_made{h}") for h in HALVES]
        x_turned = sem("x_turned")
        XT_ready = sem("XT_ready")
        R_ready = sem("R_ready")
        Z_ready = sem("Z_ready")
        l1_ready = sem("l1_ready")
        l1_copied = sem("l1_copied")
        yd_ready = sem("yd_ready")
        o_ready = sem("o_ready")

        x_rows = x.rearrange("s t d -> t s d")
        out_rows = out.rearrange("s t d -> t s d")
        w_view = "(k p) n -> p k n"
        XW_CHUNKS = GATES * 3

        block = ctx.enter_context(nc.Block())

        @block.sync
        def _(sp):
            def load_x(n, q):
                sp.dma_start(x_in[:, q, :], x_rows[bass.ds(n * BT, BT)]).then_inc(x_loaded[q], 16)

            def block_io(n, q, first=False, last=False):
                if not last:
                    sp.wait_ge(x_turned, n + 1)
                    load_x(n + 2, q)
                if not first:
                    sp.wait_ge(o_ready, n)
                    sp.dma_start(out_rows[bass.ds((n - 1) * BT, BT)], o_sb[:, 1 - q, :]).then_inc(out_stored[1 - q], 16)

            sp.dma_start(wh_sb[:], Wh.rearrange(w_view, p=P)).then_inc(wh_loaded, 16)
            sp.dma_start(wx_sb[:], Wx.rearrange(w_view, p=P)).then_inc(wx_loaded, 16)
            load_x(1, 1)
            sp.dma_start(w1_sb[:], W1.rearrange(w_view, p=P)).then_inc(w1_loaded, 16)
            block_io(0, 0, first=True)
            block_io(1, 1)
            with sp.Fori(1, NB // 2 - 1) as j:
                block_io(2 * j, 0)
                block_io(2 * j + 1, 1)
            block_io(NB - 2, 0, last=True)
            block_io(NB - 1, 1, last=True)
            sp.wait_ge(o_ready, NB)
            sp.dma_start(out_rows[(NB - 1) * BT:], o_sb[:, 1, :]).then_inc(out_stored[1], 16)
            for q in range(2):
                sp.wait_ge(out_stored[q], 16 * NB // 2)

        @block.scalar
        def _(act):
            act.dma_start(cond_sb[:], cond).then_inc(cond_loaded, 16)
            act.dma_start(x_in[:, 0, :], x_rows[0:BT]).then_inc(x_loaded[0], 16)
            act.dma_start(bias_row[:], b.rearrange("(a n) -> a n", a=1)).then_inc(b_loaded, 16)

            def copy_xT(n, q, piece):
                w = KC * P // 4
                flat = XT[:, q].rearrange("p k t s -> p (k t s)")
                ins = nc.scalar.mul(flat[:, piece * w:(piece + 1) * w], xT_ps[:, piece * w:(piece + 1) * w], 2.0)
                if piece == 3:
                    ins.then_inc(XT_ready, 1)

            def copy_l1(piece):
                w = D // 4
                at = slice(piece % 4 * w, (piece % 4 + 1) * w)
                if piece < 4:
                    nc.scalar.copy(y_sb[:, at], y_ps[:, at])
                else:
                    ins = nc.scalar.mul(r_sb[:, at], r_ps[:, at], 0.5)
                    if piece == 7:
                        ins.then_inc(l1_copied, 1)

            def side(n, q, s, first=False, last=False):
                if not last and 1 <= s <= 4:
                    if s == 1:
                        act.wait_ge(x_turned, n + 2)
                        if not first:
                            act.wait_ge(R_ready, n)
                    copy_xT(n + 1, 1 - q, s - 1)
                if not first and 6 <= s <= 13:
                    if s == 6:
                        act.wait_ge(l1_ready, n)
                        act.wait_ge(o_ready, n - 1) if not isinstance(n, int) or n > 1 else None
                    copy_l1(s - 6)

            def steps(n, q, **edge):
                for s in range(BT):
                    r = s % 2
                    for h in HALVES:
                        act.wait_ge(gates_ready[h], n * BT + s + 1)
                        nc.scalar.activation(tg[r][h][:, 0:GATES, :], gate_ps[q][h][:, :, s, :], ACT.Tanh,
                                             scale=unscale_reg).then_inc(tg_ready[h], 1)
                    for h in HALVES:
                        act.wait_ge(c_ready[h], n * BT + s + 1)
                        nc.scalar.activation(tc[r][h][:], tg[1 - r][h][:, GATES, :], ACT.Tanh,
                                             scale=0.5).then_inc(tc_ready[h], 1)
                    side(n, q, s, **edge)

            act.wait_ge(x_turned, 1)
            for piece in range(4):
                copy_xT(0, 0, piece)
            act.wait_ge(norm_ready, 1)
            nc.scalar.activation(dm_root[:], dm_v[:], ACT.Sqrt).then_inc(root_ready, 1)
            act.wait_ge(unscale_ready, 1)
            unscale_reg = ctx.enter_context(act.register("unscale_reg"))
            nc.scalar.reg_load(unscale_reg, unscale[0:1, 0:1].bitcast(I32))
            steps(0, 0, first=True)
            steps(1, 1)
            with act.Fori(1, NB // 2 - 1) as j:
                steps(2 * j, 0)
                steps(2 * j + 1, 1)
            steps(NB - 2, 0)
            steps(NB - 1, 1, last=True)
            act.wait_ge(l1_ready, NB)
            act.wait_ge(o_ready, NB - 1)
            for piece in range(8):
                copy_l1(piece)

        @block.vector
        def _(dve):
            count = [0]

            def done(ins):
                count[0] += 1
                ins.then_inc(prep, 1)
                dve.wait_ge(prep, count[0])

            nc.vector.memset(ones_row[:], 1.0).then_inc(ones_set, 1)
            for h in HALVES:
                nc.vector.memset(tg[0][h][:, GATES, :], 0.0).then_inc(c0_ready, 1)
            dve.wait_ge(wh_loaded, 16)
            nc.vector.tensor_reduce(row_max[:], wh_sb[:].rearrange("p k n -> p (k n)"), AX.X, ALU.max,
                                    apply_absolute_value=True).then_inc(max_ready, 1)
            dve.wait_ge(condT_ready, 1)
            condT = r_ps[:, 0:KC * N].rearrange("p (k s) -> p k s", k=KC)
            nc.vector.tensor_scalar(h0T[:], condT, 2.0, None, ALU.mult).then_inc(h0_ready, 1)
            done(nc.vector.tensor_scalar(ys[:], condT, float(D) ** -0.5, None, ALU.mult))
            done(nc.vector.tensor_tensor(ys_sq[:], ys[:], ys[:], ALU.mult))
            for k in range(KC):
                rep = ys_sq[:, k:k + 1, :].to_broadcast([P, BT, N])
                nc.vector.tensor_copy(ys_sq_rep[:, k], rep).then_inc(norm_in, 1)
                rep = ys[:, k:k + 1, :].to_broadcast([P, BT, N])
                nc.vector.tensor_scalar(ys_rep[:, k], rep, 0.5, None, ALU.mult).then_inc(ysq_ready, 1)
            dve.wait_ge(w1_loaded, 16)
            nc.vector.tensor_tensor(w1_sq[:], w1_sb[:], w1_sb[:], ALU.mult).then_inc(norm_in, 1)

            dve.wait_ge(norm_sums, 1)
            nc.vector.tensor_scalar(dm_v[:], y_ps[:, 0:D], EPS, None, ALU.add).then_inc(norm_ready, 1)
            dve.wait_ge(allmax_ready, 1)
            done(nc.vector.tensor_scalar(all_max_c[:], all_max[:], 2.0 ** -30, None, ALU.max))
            done(nc.vector.tensor_scalar(max_pow2[:].bitcast(I32), all_max_c[:].bitcast(I32), 0x7F800000, None,
                                         ALU.bitwise_and))
            nc.vector.tensor_scalar(unscale[:], max_pow2[:], 2.0 ** -14, None, ALU.mult).then_inc(unscale_ready, 1)
            done(nc.vector.reciprocal(inv_pow2[:], max_pow2[:]))
            nc.vector.tensor_scalar(scale_ifo[:], inv_pow2[:], 0.25 * 2.0 ** 14, None, ALU.mult)
            nc.vector.tensor_scalar(scale_b[:], inv_pow2[:], 2.0 ** 14, None, ALU.mult)
            done(nc.vector.tensor_scalar(scale_g[:], inv_pow2[:], 0.5 * 2.0 ** 14, None, ALU.mult))
            IFO = 3 * HID
            dve.wait_ge(wx_loaded, 16)
            nc.vector.tensor_scalar(wx_sb[:, :, 0:IFO], wx_sb[:, :, 0:IFO], scale_ifo[:], None, ALU.mult)
            nc.vector.tensor_scalar(wx_sb[:, :, IFO:G4], wx_sb[:, :, IFO:G4], scale_g[:], None,
                                    ALU.mult).then_inc(wx_scaled, 1)
            dve.wait_ge(b_loaded, 16)
            nc.vector.tensor_scalar(bias_scaled[:, 0:IFO], bias_row[:, 0:IFO], scale_b[0:1, :], 0.5, ALU.mult, ALU.mult)
            nc.vector.tensor_scalar(bias_scaled[:, IFO:G4], bias_row[:, IFO:G4], scale_b[0:1, :], None,
                                    ALU.mult).then_inc(bias_ready, 1)
            nc.vector.tensor_scalar(wh_sb[:, :, 0:IFO], wh_sb[:, :, 0:IFO], scale_ifo[:], None, ALU.mult)
            nc.vector.tensor_scalar(wh_sb[:, :, IFO:G4], wh_sb[:, :, IFO:G4], scale_g[:], None,
                                    ALU.mult).then_inc(wh_scaled, 1)
            dve.wait_ge(wh_scaled, 1)
            nc.vector.tensor_copy(wh_hi[:], wh_sb[:]).then_inc(hi_ready, 1)
            dve.wait_ge(hi_ready, 1)
            nc.vector.tensor_tensor(wh_lo[:], wh_sb[:], wh_hi[:], ALU.subtract).then_inc(split_ready, 1)
            dve.wait_ge(root_ready, 1)
            done(nc.vector.reciprocal(dm_a[:], dm_root[:]))
            done(nc.vector.tensor_tensor(dm_b[:], dm_a[:], dm_a[:], ALU.mult))
            done(nc.vector.tensor_tensor(dm_b[:], dm_b[:], dm_v[:], ALU.mult))
            done(nc.vector.tensor_scalar(dm_b[:], dm_b[:], -0.5, 1.5, ALU.mult, ALU.add))
            nc.vector.tensor_tensor(demod[:], dm_a[:], dm_b[:], ALU.mult).then_inc(demod_ready, 1)

            def cell(n, h, s):
                r = s % 2
                dve.wait_ge(tg_ready[h], n * BT + s + 1)
                nc.vector.scalar_tensor_tensor(out=uv[r][h][:], in0=tg[r][h][:, 0:2, :], scalar=1.0,
                                               in1=tg[r][h][:, 3:5, :], op0=ALU.add,
                                               op1=ALU.mult).then_inc(uv_ready[h], 1)
                dve.wait_ge(uv_ready[h], n * BT + s + 1)
                nc.vector.scalar_tensor_tensor(out=tg[1 - r][h][:, GATES, :], in0=uv[r][h][:, 1, :], scalar=0.5,
                                               in1=uv[r][h][:, 0, :], op0=ALU.mult,
                                               op1=ALU.add).then_inc(c_ready[h], 1)

            def hidden(n, q, h, s):
                r = s % 2
                dve.wait_ge(tc_ready[h], n * BT + s + 1)
                tanh_o = tg[r][h][:, 2, :]
                H_s = H_all[:, q, h, s, :]
                nc.vector.scalar_tensor_tensor(out=H_hi[r][h][:], in0=tanh_o, scalar=1.0, in1=tc[r][h][:],
                                               op0=ALU.add, op1=ALU.mult).then_inc(hi_made[h], 1)
                nc.vector.scalar_tensor_tensor(out=H_s, in0=tanh_o, scalar=1.0, in1=tc[r][h][:],
                                               op0=ALU.add, op1=ALU.mult).then_inc(full_made[h], 1)
                dve.wait_ge(hi_made[h], n * BT + s + 1)
                dve.wait_ge(full_made[h], n * BT + s + 1)
                nc.vector.tensor_tensor(H_lo[r][h][:], H_s, H_hi[r][h][:], ALU.subtract).then_inc(lo_made[h], 1)

            def steps(n, q, first=False):
                for s in range(BT):
                    for h in HALVES:
                        cell(n, h, s)
                    if s == 0 and not first and not (isinstance(n, int) and n < 2):
                        dve.wait_ge(R_ready, n - 1)
                    for h in HALVES:
                        hidden(n, q, h, s)

            dve.wait_ge(c0_ready, 2)
            steps(0, 0, first=True)
            steps(1, 1)
            with dve.Fori(1, NB // 2 - 1) as j:
                steps(2 * j, 0)
                steps(2 * j + 1, 1)
            steps(NB - 2, 0)
            steps(NB - 1, 1)

        @block.gpsimd
        def _(pool):
            nc.gpsimd.memset(ident[:], 0.0).then_inc(ident_zero, 1)
            pool.wait_ge(ident_zero, 1)
            nc.gpsimd.affine_select(out=ident[:], in_=ident[:], compare_op=ALU.not_equal, fill=1.0, base=0,
                                    pattern=[[-1, P]], channel_multiplier=1).then_inc(ident_ready, 1)
            pool.wait_ge(max_ready, 1)
            nc.gpsimd.partition_all_reduce(all_max[:], row_max[:], P, bass.bass_isa.ReduceOp.max).then_inc(allmax_ready, 1)

            def modulate(n, q):
                for h in HALVES:
                    pool.wait_ge(full_made[h], (n + 1) * BT)
                if not isinstance(n, int) or n > 0:
                    pool.wait_ge(l1_ready, n)
                flat = "p k t s -> p (k t s)"
                Rf = R[:].rearrange("p k m -> p (k m)")
                nc.gpsimd.tensor_tensor(Rf, H_all[:, q].rearrange(flat), XT[:, q].rearrange(flat),
                                        ALU.add).then_inc(R_ready, 1)
                pool.wait_ge(R_ready, n + 1)
                nc.gpsimd.tensor_tensor(Z[:].rearrange("p k m -> p (k m)"), Rf, ys_rep[:].rearrange(flat),
                                        ALU.mult).then_inc(Z_ready, 1)

            def finish(n, q):
                pool.wait_ge(l1_copied, n + 1)
                nc.gpsimd.tensor_tensor(yd_sb[:], y_sb[:], demod[:], ALU.mult).then_inc(yd_ready, 1)
                pool.wait_ge(yd_ready, n + 1)
                if not isinstance(n, int) or n > 1:
                    pool.wait_ge(out_stored[q], 8 * (n - q))
                nc.gpsimd.tensor_tensor(o_sb[:, q, :], yd_sb[:], r_sb[:], ALU.add).then_inc(o_ready, 1)

            pool.wait_ge(ysq_ready, 2)
            pool.wait_ge(demod_ready, 1)
            for n in range(2):
                modulate(n, n)
                finish(n, n)
            with pool.Fori(1, NB // 2 - 1) as j:
                for q in range(2):
                    modulate(2 * j + q, q)
                    finish(2 * j + q, q)
            for n in range(NB - 2, NB):
                modulate(n, n % 2)
                finish(n, n % 2)

        @block.tensor
        def _(pe):
            def turn_x(n, q):
                pe.wait_ge(x_loaded[q], 8 * (n - q) + 16)
                for k in range(KC):
                    ins = nc.tensor.transpose(xT_ps[:, k * P:(k + 1) * P], x_in[:, q, k * P:(k + 1) * P], ident[:])
                ins.then_inc(x_turned, 1)

            def gates_from_x(q, h, piece):
                gate, what = divmod(piece, 3)
                cols = slice(gate * HID + h * P, gate * HID + (h + 1) * P)
                to = gate_ps[q][h][:, gate].rearrange("p t s -> p (t s)")
                if what < KC:
                    nc.tensor.matmul(to, wx_sb[:, what, cols], XT[:, q, what].rearrange("p t s -> p (t s)"),
                                     start=(piece == 0), stop=False, skip_group_check=True)
                else:
                    nc.tensor.matmul(to, bias_scaled[:, cols], ones_row[:], start=False, stop=True,
                                     skip_group_check=True)

            def l1_products():
                for k in range(KC):
                    nc.tensor.matmul(y_ps[:, 0:D], Z[:, k], w1_sb[:, k, :], start=(k == 0), stop=(k == KC - 1))

            def l1_turn():
                for k in range(KC):
                    ins = nc.tensor.transpose(r_ps[:, k * P:(k + 1) * P], R[:, k], ident[:])
                ins.then_inc(l1_ready, 1)

            def side(n, q, s, first=False, last=False):
                if not last:
                    if s == 0:
                        turn_x(n + 1, 1 - q)
                    if s == 5:
                        pe.wait_ge(XT_ready, n + 2)
                    if 5 <= s < 13:
                        for piece in range(3 * (s - 5), 3 * (s - 4)):
                            gates_from_x(1 - q, piece // XW_CHUNKS, piece % XW_CHUNKS)
                if not first:
                    if s == 2:
                        pe.wait_ge(Z_ready, n)
                        if not isinstance(n, int) or n > 1:
                            pe.wait_ge(l1_copied, n - 1)
                        l1_products()
                    if s == 3:
                        l1_turn()

            def recurrence(n, q, s):
                r = (s - 1) % 2
                t = n * BT + s

                def products(k, h, part, w, last=False):
                    for gate in range(GATES):
                        cols = slice(gate * HID + h * P, gate * HID + (h + 1) * P)
                        ins = nc.tensor.matmul(gate_ps[q][h][:, gate, s, :], w[:, k, cols], part[r][k][:],
                                               start=False, stop=last, skip_group_check=True)
                    return ins

                pe.wait_ge(hi_made[0], t)
                products(0, 0, H_hi, wh_hi)
                products(0, 0, H_hi, wh_lo)
                pe.wait_ge(tg_ready[1], t)
                products(0, 1, H_hi, wh_hi)
                products(0, 1, H_hi, wh_lo)
                pe.wait_ge(lo_made[0], t)
                products(0, 0, H_lo, wh_hi)
                products(0, 1, H_lo, wh_hi)
                for h in HALVES:
                    if h == 0:
                        pe.wait_ge(hi_made[1], t)
                    products(1, h, H_hi, wh_hi)
                    products(1, h, H_hi, wh_lo)
                    if h == 0:
                        pe.wait_ge(lo_made[1], t)
                    products(1, h, H_lo, wh_hi, last=True).then_inc(gates_ready[h], 1)

            def steps(n, q, **edge):
                for s in range(BT):
                    if edge.get("first") and s == 0:
                        first_step()
                    else:
                        recurrence(n, q, s)
                    side(n, q, s, **edge)

            def first_step():
                pe.wait_ge(wh_scaled, 1)
                pe.wait_ge(h0_ready, 1)
                for h in HALVES:
                    for gate in range(GATES):
                        cols = slice(gate * HID + h * P, gate * HID + (h + 1) * P)
                        for k in range(KC):
                            ins = nc.tensor.matmul(gate_ps[0][h][:, gate, 0, :], wh_sb[:, k, cols], h0T[:, k, :],
                                                   start=False, stop=(k == KC - 1), skip_group_check=True)
                    ins.then_inc(gates_ready[h], 1)
                pe.wait_ge(split_ready, 1)

            pe.wait_ge(ident_ready, 1)
            pe.wait_ge(cond_loaded, 16)
            for k in range(KC):
                ins = nc.tensor.transpose(r_ps[:, k * N:(k + 1) * N], cond_sb[:, k * P:(k + 1) * P], ident[0:N, 0:N])
            ins.then_inc(condT_ready, 1)
            turn_x(0, 0)
            pe.wait_ge(norm_in, 3)
            for k in range(KC):
                ins = nc.tensor.matmul(y_ps[:, 0:D], ys_sq_rep[:, k].rearrange("p t s -> p (t s)"), w1_sq[:, k, :],
                                       start=(k == 0), stop=(k == KC - 1))
            ins.then_inc(norm_sums, 1)
            pe.wait_ge(wx_scaled, 1)
            pe.wait_ge(bias_ready, 1)
            pe.wait_ge(ones_set, 1)
            pe.wait_ge(XT_ready, 1)
            for h in HALVES:
                for piece in range(XW_CHUNKS):
                    gates_from_x(0, h, piece)
            steps(0, 0, first=True)
            steps(1, 1)
            with pe.Fori(1, NB // 2 - 1) as j:
                steps(2 * j, 0)
                steps(2 * j + 1, 1)
            steps(NB - 2, 0)
            steps(NB - 1, 1, last=True)
            pe.wait_ge(Z_ready, NB)
            pe.wait_ge(l1_copied, NB - 1)
            l1_products()
            l1_turn()


_INS = ['x', 'cond_1024', 'L0_cond_Wx', 'L0_cond_Wh', 'L0_cond_b', 'L1_cond_weight']
_OUTS = [((8, 256, 256), 'float32')]


def kernel(**inputs):
    import numpy as _np
    import concourse.bacc as _bacc
    from concourse import mybir as _mybir
    from concourse.bass_utils import run_bass_kernel_spmd as _run

    nc = _bacc.Bacc("TRN2", target_bir_lowering=False, num_devices=1)
    arrays, args = {}, []
    for name in _INS:
        a = _np.ascontiguousarray(inputs[name])
        arrays[f"in_{name}_dram"] = a
        args.append(nc.dram_tensor(f"in_{name}_dram", a.shape, _mybir.dt.from_np(a.dtype), kind="ExternalInput").ap())
    for i, (shape, dtype) in enumerate(_OUTS):
        dt = _mybir.dt.from_np(_np.dtype(dtype))
        args.append(nc.dram_tensor(f"out_{i}_dram", shape, dt, kind="ExternalOutput").ap())
    lstm_modulated_residual(nc, *args)
    r = _run(nc, [arrays], core_ids=[0])
    got = tuple(r.results[0][f"out_{i}_dram"] for i in range(len(_OUTS)))
    return got[0]
```

```python
import concourse.bass as bass
from concourse import mybir
from contextlib import ExitStack

F32 = mybir.dt.float32
F16 = mybir.dt.float16
BF16 = mybir.dt.bfloat16
I32 = mybir.dt.int32
ALU = mybir.AluOpType
ACT = mybir.ActivationFunctionType
AX = mybir.AxisListType

P = 128
BT = 16
GATES = 4
EPS = 1e-8
WIN = 4
L0 = 2


def lstm_modulated_residual(
    nc: bass.Bass,
    x: bass.AP,
    cond: bass.AP,
    Wx: bass.AP,
    Wh: bass.AP,
    b: bass.AP,
    W1: bass.AP,
    out: bass.AP,
):
    N, T, D = x.shape
    HID = D
    KC = D // P
    NB = T // BT
    G4 = GATES * HID
    assert N * BT == P and D == 2 * P and NB % 2 == 0 and NB >= 6
    HALVES = range(KC)

    ctx = ExitStack()
    with ctx:
        def sb(name, shape, dt=F32):
            return ctx.enter_context(nc.sbuf_tensor(name, shape, dt))

        def pb(name, shape, dt=F32):
            return ctx.enter_context(nc.psum_tensor(name, shape, dt))

        def sem(name):
            return ctx.enter_context(nc.semaphore(name))

        wx_sb = sb("wx_sb", [P, KC, G4])
        wh_sb = sb("wh_sb", [P, KC, G4])
        wh_hi = sb("wh_hi", [P, KC, G4], F16)
        wh_lo = sb("wh_lo", [P, KC, G4], F16)
        w1_sb = sb("w1_sb", [P, KC, D])
        w1_sq = sb("w1_sq", [P, KC, D])
        QUAD = 32
        bias_rep = sb("bias_rep", [3 * QUAD, G4])
        bias_rest = sb("bias_rest", [3 * QUAD, G4])
        bias_parts = sb("bias_parts", [3 * QUAD, G4], BF16)
        bias_tmp = sb("bias_tmp", [3 * QUAD, G4], BF16)
        ones_col = sb("ones_col", [3 * QUAD, P], BF16)
        ident = sb("ident", [P, P])
        row_max = sb("row_max", [P, 1])
        all_max = sb("all_max", [P, 1])
        all_max_c = sb("all_max_c", [P, 1])
        max_pow2 = sb("max_pow2", [P, 1])
        inv_pow2 = sb("inv_pow2", [P, 1])
        scale_ifo = sb("scale_ifo", [P, 1])
        scale_g = sb("scale_g", [P, 1])
        scale_b = sb("scale_b", [P, 1])
        unscale = sb("unscale", [P, 1])
        cond_sb = sb("cond_sb", [N, D])
        h0T = sb("h0T", [P, KC, N])
        ys = sb("ys", [P, KC, N])
        ys_sq = sb("ys_sq", [P, KC, N])
        ys_rep = sb("ys_rep", [P, KC, BT, N])
        ys_sq_rep = sb("ys_sq_rep", [P, KC, BT, N])
        demod = sb("demod", [P, D])
        dm_v = sb("dm_v", [P, D])
        dm_root = sb("dm_root", [P, D])
        dm_a = sb("dm_a", [P, D])
        dm_b = sb("dm_b", [P, D])
        x_in = sb("x_in", [P, 2, D])
        XT = sb("XT", [P, 2, KC, BT, N])
        H_all = sb("H_all", [P, 2, KC, BT, N])
        XR = sb("XR", [P, KC, P])
        R = sb("R", [P, KC, P])
        Z = sb("Z", [P, KC, P])
        y_sb = sb("y_sb", [P, D])
        r_sb = sb("r_sb", [P, D])
        yd_sb = sb("yd_sb", [P, D])
        o_sb = sb("o_sb", [P, 2, D])
        tg = [[sb(f"tg{q}{h}", [P, 4, N]) for h in HALVES] for q in range(2)]
        to = [sb(f"to{q}", [P, KC, N]) for q in range(2)]
        uv = [[sb(f"uv{q}{h}", [P, 2, N]) for h in HALVES] for q in range(2)]
        tc = [[sb(f"tc{q}{h}", [P, N]) for h in HALVES] for q in range(2)]
        H_hi = [sb(f"H_hi{h}", [P, WIN, WIN, N], F16) for h in HALVES]
        H_lo = [sb(f"H_lo{h}", [P, WIN, WIN, N], F16) for h in HALVES]

        ifg_ps = [[pb(f"ifg_ps{q}{h}", [P, 4, BT, N]) for h in HALVES] for q in range(2)]
        o_ps = [pb(f"o_ps{q}", [P, 2 * KC, BT, N]) for q in range(2)]
        turn_ps = pb("turn_ps", [P, 512])
        xT_ps = turn_ps[:, 0:KC * P]
        r_ps = turn_ps[:, KC * P:2 * KC * P]
        y_ps = pb("y_ps", [P, 512])

        x_loaded = [sem(f"x_loaded{q}") for q in range(2)]
        wx_loaded = sem("wx_loaded")
        wh_loaded = sem("wh_loaded")
        b_loaded = sem("b_loaded")
        w1_loaded = sem("w1_loaded")
        cond_loaded = sem("cond_loaded")
        out_stored = [sem(f"out_stored{q}") for q in range(2)]
        ones_set = sem("ones_set")
        ident_zero = sem("ident_zero")
        ident_ready = sem("ident_ready")
        prep = sem("prep")
        max_ready = sem("max_ready")
        allmax_ready = sem("allmax_ready")
        unscale_ready = sem("unscale_ready")
        condT_ready = sem("condT_ready")
        h0_ready = sem("h0_ready")
        wx_scaled = sem("wx_scaled")
        bias_ready = sem("bias_ready")
        wh_scaled = sem("wh_scaled")
        hi_ready = sem("hi_ready")
        split_ready = sem("split_ready")
        c0_ready = sem("c0_ready")
        ysq_ready = sem("ysq_ready")
        norm_ready = sem("norm_ready")
        root_ready = sem("root_ready")
        demod_ready = sem("demod_ready")
        norm_in = sem("norm_in")
        norm_sums = sem("norm_sums")
        gates_ready = [sem(f"gates_ready{h}") for h in HALVES]
        tg_ready = [sem(f"tg_ready{h}") for h in HALVES]
        o_summed = sem("o_summed")
        uv_ready = [sem(f"uv_ready{h}") for h in HALVES]
        c_ready = [sem(f"c_ready{h}") for h in HALVES]
        tc_ready = [sem(f"tc_ready{h}") for h in HALVES]
        hi_made = [sem(f"hi_made{h}") for h in HALVES]
        full_made = [sem(f"full_made{h}") for h in HALVES]
        lo_made = [sem(f"lo_made{h}") for h in HALVES]
        x_turned = sem("x_turned")
        XT_ready = sem("XT_ready")
        XR_ready = sem("XR_ready")
        R_ready = sem("R_ready")
        Z_ready = sem("Z_ready")
        l1_ready = sem("l1_ready")
        l1_copied = sem("l1_copied")
        yd_ready = sem("yd_ready")
        o_ready = sem("o_ready")

        x_rows = x.rearrange("s t d -> t s d")
        out_rows = out.rearrange("s t d -> t s d")
        w_view = "(k p) n -> p k n"
        XW_CHUNKS = GATES * 3

        block = ctx.enter_context(nc.Block())

        @block.sync
        def _(sp):
            def load_x(n, q):
                sp.dma_start(x_in[:, q, :], x_rows[bass.ds(n * BT, BT)]).then_inc(x_loaded[q], 16)

            def block_io(n, q, first=False, ahead=2):
                if ahead >= 2:
                    sp.wait_ge(x_turned, n + 1)
                    load_x(n + 2, q)
                if not first:
                    sp.wait_ge(o_ready, n)
                    sp.dma_start(out_rows[bass.ds((n - 1) * BT, BT)], o_sb[:, 1 - q, :]).then_inc(out_stored[1 - q], 16)

            sp.dma_start(wh_sb[:], Wh.rearrange(w_view, p=P)).then_inc(wh_loaded, 16)
            sp.dma_start(wx_sb[:], Wx.rearrange(w_view, p=P)).then_inc(wx_loaded, 16)
            load_x(1, 1)
            sp.dma_start(w1_sb[:], W1.rearrange(w_view, p=P)).then_inc(w1_loaded, 16)
            block_io(0, 0, first=True)
            block_io(1, 1)
            with sp.Fori(1, NB // 2 - 1) as j:
                block_io(2 * j, 0)
                block_io(2 * j + 1, 1)
            block_io(NB - 2, 0, ahead=1)
            block_io(NB - 1, 1, ahead=0)
            sp.wait_ge(o_ready, NB)
            sp.dma_start(out_rows[(NB - 1) * BT:], o_sb[:, 1, :]).then_inc(out_stored[1], 16)
            for q in range(2):
                sp.wait_ge(out_stored[q], 16 * NB // 2)

        @block.scalar
        def _(act):
            act.dma_start(cond_sb[:], cond).then_inc(cond_loaded, 16)
            act.dma_start(x_in[:, 0, :], x_rows[0:BT]).then_inc(x_loaded[0], 16)
            for i in range(3):
                act.dma_start(bias_rep[QUAD * i:QUAD * i + 1, :], b.rearrange("(a n) -> a n", a=1)).then_inc(b_loaded, 16)

            def copy_xT(n, q, piece):
                w = KC * P // 4
                flat = XT[:, q].rearrange("p k t s -> p (k t s)")
                ins = nc.scalar.mul(flat[:, piece * w:(piece + 1) * w], xT_ps[:, piece * w:(piece + 1) * w], 2.0)
                if piece == 3:
                    ins.then_inc(XT_ready, 1)

            def copy_l1(piece):
                w = D // 4
                at = slice(piece % 4 * w, (piece % 4 + 1) * w)
                if piece < 4:
                    nc.scalar.copy(y_sb[:, at], y_ps[:, at])
                else:
                    ins = nc.scalar.mul(r_sb[:, at], r_ps[:, at], 0.5)
                    if piece == 7:
                        ins.then_inc(l1_copied, 1)

            def side(n, q, s, first=False, ahead=2):
                if not first and 7 <= s < 11:
                    if s == 7:
                        if not isinstance(n, int) or n > 1:
                            act.wait_ge(o_ready, n - 1)
                        act.wait_ge(l1_ready, n)
                    copy_l1(2 * (s - 7))
                    copy_l1(2 * (s - 7) + 1)
                if ahead >= 2 and 12 <= s < 14:
                    if s == 12:
                        act.wait_ge(XR_ready, n + 1)
                        act.wait_ge(x_turned, n + 3)
                    copy_xT(n + 2, q, 2 * (s - 12))
                    copy_xT(n + 2, q, 2 * (s - 12) + 1)

            def steps(n, q, **edge):
                for s in range(BT):
                    r = s % 2
                    for h in HALVES:
                        act.wait_ge(gates_ready[h], n * BT + s + 1)
                        nc.scalar.activation(tg[r][h][:, 0:3, :], ifg_ps[q][h][:, 0:3, s, :], ACT.Tanh,
                                             scale=unscale_reg).then_inc(tg_ready[h], 1)
                    act.wait_ge(o_summed, n * BT + s + 1)
                    nc.scalar.activation(to[r][:], o_ps[q][:, 0:KC, s, :], ACT.Tanh,
                                         scale=unscale_reg)
                    for h in HALVES:
                        act.wait_ge(c_ready[h], n * BT + s + 1)
                        nc.scalar.activation(tc[r][h][:], tg[1 - r][h][:, 3, :], ACT.Tanh,
                                             scale=0.5).then_inc(tc_ready[h], 1)
                    side(n, q, s, **edge)

            for n in range(2):
                act.wait_ge(x_turned, n + 1)
                for piece in range(4):
                    copy_xT(n, n, piece)
            act.wait_ge(norm_ready, 1)
            nc.scalar.activation(dm_root[:], dm_v[:], ACT.Sqrt).then_inc(root_ready, 1)
            act.wait_ge(unscale_ready, 1)
            unscale_reg = ctx.enter_context(act.register("unscale_reg"))
            nc.scalar.reg_load(unscale_reg, unscale[0:1, 0:1].bitcast(I32))
            steps(0, 0, first=True)
            steps(1, 1)
            with act.Fori(1, NB // 2 - 1) as j:
                steps(2 * j, 0)
                steps(2 * j + 1, 1)
            steps(NB - 2, 0, ahead=1)
            steps(NB - 1, 1, ahead=0)
            act.wait_ge(l1_ready, NB)
            act.wait_ge(o_ready, NB - 1)
            for piece in range(8):
                copy_l1(piece)

        @block.vector
        def _(dve):
            count = [0]

            def done(ins):
                count[0] += 1
                ins.then_inc(prep, 1)
                dve.wait_ge(prep, count[0])

            nc.vector.memset(ones_col[:], 1.0).then_inc(ones_set, 1)
            nc.vector.memset(bias_parts[:].bitcast(I32), 0).then_inc(ones_set, 1)
            for h in HALVES:
                nc.vector.memset(tg[0][h][:, 3, :], 0.0).then_inc(c0_ready, 1)
                for part in (H_hi, H_lo):
                    nc.vector.memset(part[h][:].rearrange("p w t s -> p (w t s)").bitcast(I32), 0).then_inc(c0_ready, 1)
            dve.wait_ge(wh_loaded, 16)
            nc.vector.tensor_reduce(row_max[:], wh_sb[:].rearrange("p k n -> p (k n)"), AX.X, ALU.max,
                                    apply_absolute_value=True).then_inc(max_ready, 1)
            dve.wait_ge(condT_ready, 1)
            condT = y_ps[:, 0:KC * N].rearrange("p (k s) -> p k s", k=KC)
            nc.vector.tensor_scalar(h0T[:], condT, 2.0, None, ALU.mult).then_inc(h0_ready, 1)
            done(nc.vector.tensor_scalar(ys[:], condT, float(D) ** -0.5, None, ALU.mult))
            done(nc.vector.tensor_tensor(ys_sq[:], ys[:], ys[:], ALU.mult))
            for k in range(KC):
                rep = ys_sq[:, k:k + 1, :].to_broadcast([P, BT, N])
                nc.vector.tensor_copy(ys_sq_rep[:, k], rep).then_inc(norm_in, 1)
                rep = ys[:, k:k + 1, :].to_broadcast([P, BT, N])
                nc.vector.tensor_scalar(ys_rep[:, k], rep, 0.5, None, ALU.mult).then_inc(ysq_ready, 1)
            dve.wait_ge(w1_loaded, 16)
            nc.vector.tensor_tensor(w1_sq[:], w1_sb[:], w1_sb[:], ALU.mult).then_inc(norm_in, 1)

            dve.wait_ge(norm_sums, 1)
            nc.vector.tensor_scalar(dm_v[:], y_ps[:, 0:D], EPS, None, ALU.add).then_inc(norm_ready, 1)
            dve.wait_ge(allmax_ready, 1)
            done(nc.vector.tensor_scalar(all_max_c[:], all_max[:], 2.0 ** -30, None, ALU.max))
            done(nc.vector.tensor_scalar(max_pow2[:].bitcast(I32), all_max_c[:].bitcast(I32), 0x7F800000, None,
                                         ALU.bitwise_and))
            nc.vector.tensor_scalar(unscale[:], max_pow2[:], 2.0 ** -14, None, ALU.mult).then_inc(unscale_ready, 1)
            done(nc.vector.reciprocal(inv_pow2[:], max_pow2[:]))
            nc.vector.tensor_scalar(scale_ifo[:], inv_pow2[:], 0.25 * 2.0 ** 14, None, ALU.mult)
            nc.vector.tensor_scalar(scale_b[:], inv_pow2[:], 2.0 ** 14, None, ALU.mult)
            done(nc.vector.tensor_scalar(scale_g[:], inv_pow2[:], 0.5 * 2.0 ** 14, None, ALU.mult))
            IFO = 3 * HID
            dve.wait_ge(wx_loaded, 16)
            nc.vector.tensor_scalar(wx_sb[:, :, 0:IFO], wx_sb[:, :, 0:IFO], scale_ifo[:], None, ALU.mult)
            nc.vector.tensor_scalar(wx_sb[:, :, IFO:G4], wx_sb[:, :, IFO:G4], scale_g[:], None,
                                    ALU.mult).then_inc(wx_scaled, 1)
            dve.wait_ge(b_loaded, 48)
            dve.wait_ge(ones_set, 2)
            for i in range(3):
                row = slice(QUAD * i, QUAD * i + 1)
                nc.vector.tensor_scalar(bias_rep[row, 0:IFO], bias_rep[row, 0:IFO], scale_b[row, :], 0.5, ALU.mult, ALU.mult)
                done(nc.vector.tensor_scalar(bias_rep[row, IFO:G4], bias_rep[row, IFO:G4], scale_b[row, :], None, ALU.mult))
                rest = bias_rep
                for _ in range(i):
                    done(nc.vector.tensor_copy(bias_tmp[row, :], rest[row, :]))
                    done(nc.vector.tensor_tensor(bias_rest[row, :], rest[row, :], bias_tmp[row, :], ALU.subtract))
                    rest = bias_rest
                nc.vector.tensor_copy(bias_parts[row, :], rest[row, :]).then_inc(bias_ready, 1)
            nc.vector.tensor_scalar(wh_sb[:, :, 0:IFO], wh_sb[:, :, 0:IFO], scale_ifo[:], None, ALU.mult)
            nc.vector.tensor_scalar(wh_sb[:, :, IFO:G4], wh_sb[:, :, IFO:G4], scale_g[:], None,
                                    ALU.mult).then_inc(wh_scaled, 1)
            dve.wait_ge(wh_scaled, 1)
            nc.vector.tensor_copy(wh_hi[:], wh_sb[:]).then_inc(hi_ready, 1)
            dve.wait_ge(hi_ready, 1)
            nc.vector.tensor_tensor(wh_lo[:], wh_sb[:], wh_hi[:], ALU.subtract).then_inc(split_ready, 1)
            dve.wait_ge(root_ready, 1)
            done(nc.vector.reciprocal(dm_a[:], dm_root[:]))
            done(nc.vector.tensor_tensor(dm_b[:], dm_a[:], dm_a[:], ALU.mult))
            done(nc.vector.tensor_tensor(dm_b[:], dm_b[:], dm_v[:], ALU.mult))
            done(nc.vector.tensor_scalar(dm_b[:], dm_b[:], -0.5, 1.5, ALU.mult, ALU.add))
            nc.vector.tensor_tensor(demod[:], dm_a[:], dm_b[:], ALU.mult).then_inc(demod_ready, 1)

            def cell(n, h, s):
                r = s % 2
                dve.wait_ge(tg_ready[h], n * BT + s + 1)
                nc.vector.scalar_tensor_tensor(out=uv[r][h][:], in0=tg[r][h][:, 0:2, :], scalar=1.0,
                                               in1=tg[r][h][:, 2:4, :], op0=ALU.add,
                                               op1=ALU.mult).then_inc(uv_ready[h], 1)
                dve.wait_ge(uv_ready[h], n * BT + s + 1)
                nc.vector.scalar_tensor_tensor(out=tg[1 - r][h][:, 3, :], in0=uv[r][h][:, 1, :], scalar=0.5,
                                               in1=uv[r][h][:, 0, :], op0=ALU.mult,
                                               op1=ALU.add).then_inc(c_ready[h], 1)

            def hidden_hi(n, h, s):
                r = s % 2
                dve.wait_ge(tc_ready[h], n * BT + s + 1)
                w = (s + 1) % WIN
                nc.vector.scalar_tensor_tensor(out=H_hi[h][:, w, w, :], in0=to[r][:, h, :], scalar=1.0, in1=tc[r][h][:],
                                               op0=ALU.add, op1=ALU.mult).then_inc(hi_made[h], 1)

            def hidden(n, q, h, s):
                r = s % 2
                nc.vector.scalar_tensor_tensor(out=H_all[:, q, h, s, :], in0=to[r][:, h, :], scalar=1.0, in1=tc[r][h][:],
                                               op0=ALU.add, op1=ALU.mult).then_inc(full_made[h], 1)

            def hidden_lo(n, q, h, s):
                w = (s + 1) % WIN
                dve.wait_ge(full_made[h], n * BT + s + 1)
                nc.vector.tensor_tensor(H_lo[h][:, w, w, :], H_all[:, q, h, s, :], H_hi[h][:, w, w, :],
                                        ALU.subtract).then_inc(lo_made[h], 1)

            def steps(n, q, first=False):
                for s in range(BT):
                    for h in HALVES:
                        cell(n, h, s)
                    if s == 0 and not first and not (isinstance(n, int) and n < 2):
                        dve.wait_ge(R_ready, n - 1)
                    hidden_hi(n, 0, s)
                    hidden(n, q, 0, s)
                    hidden_hi(n, 1, s)
                    hidden(n, q, 1, s)
                    hidden_lo(n, q, 0, s)
                    hidden_lo(n, q, 1, s)

            dve.wait_ge(c0_ready, 2 + 2 * KC)
            steps(0, 0, first=True)
            steps(1, 1)
            with dve.Fori(1, NB // 2 - 1) as j:
                steps(2 * j, 0)
                steps(2 * j + 1, 1)
            steps(NB - 2, 0)
            steps(NB - 1, 1)

        @block.gpsimd
        def _(pool):
            nc.gpsimd.memset(ident[:], 0.0).then_inc(ident_zero, 1)
            pool.wait_ge(ident_zero, 1)
            nc.gpsimd.affine_select(out=ident[:], in_=ident[:], compare_op=ALU.not_equal, fill=1.0, base=0,
                                    pattern=[[-1, P]], channel_multiplier=1).then_inc(ident_ready, 1)
            pool.wait_ge(max_ready, 1)
            nc.gpsimd.partition_all_reduce(all_max[:], row_max[:], P, bass.bass_isa.ReduceOp.max).then_inc(allmax_ready, 1)

            def modulate(n, q, last=False):
                if not last:
                    pool.wait_ge(XT_ready, n + 2)
                for h in HALVES:
                    pool.wait_ge(full_made[h], (n + 1) * BT)
                if not isinstance(n, int) or n > 0:
                    pool.wait_ge(l1_ready, n)
                flat = "p k t s -> p (k t s)"
                Rf = R[:].rearrange("p k m -> p (k m)")
                pool.wait_ge(XR_ready, n + 1)
                nc.gpsimd.tensor_tensor(Rf, H_all[:, q].rearrange(flat), XR[:].rearrange("p k m -> p (k m)"),
                                        ALU.add).then_inc(R_ready, 1)
                pool.wait_ge(R_ready, n + 1)
                nc.gpsimd.tensor_tensor(Z[:].rearrange("p k m -> p (k m)"), Rf, ys_rep[:].rearrange(flat),
                                        ALU.mult).then_inc(Z_ready, 1)
                if not last:
                    keep_x(1 - q)

            def keep_x(q):
                nc.gpsimd.tensor_copy(XR[:].rearrange("p k m -> p (k m)"),
                                      XT[:, q].rearrange("p k t s -> p (k t s)")).then_inc(XR_ready, 1)

            def finish(n, q):
                pool.wait_ge(l1_copied, n + 1)
                nc.gpsimd.tensor_tensor(yd_sb[:], y_sb[:], demod[:], ALU.mult).then_inc(yd_ready, 1)
                pool.wait_ge(yd_ready, n + 1)
                if not isinstance(n, int) or n > 1:
                    pool.wait_ge(out_stored[q], 8 * (n - q))
                nc.gpsimd.tensor_tensor(o_sb[:, q, :], yd_sb[:], r_sb[:], ALU.add).then_inc(o_ready, 1)

            pool.wait_ge(XT_ready, 1)
            keep_x(0)
            pool.wait_ge(ysq_ready, 2)
            pool.wait_ge(demod_ready, 1)
            for n in range(2):
                modulate(n, n)
                finish(n, n)
            with pool.Fori(1, NB // 2 - 1) as j:
                for q in range(2):
                    modulate(2 * j + q, q)
                    finish(2 * j + q, q)
            modulate(NB - 2, 0)
            finish(NB - 2, 0)
            modulate(NB - 1, 1, last=True)
            finish(NB - 1, 1)

        @block.tensor
        def _(pe):
            def turn_x(n, q):
                pe.wait_ge(x_loaded[q], 8 * (n - q) + 16)
                for k in range(KC):
                    ins = nc.tensor.transpose(xT_ps[:, k * P:(k + 1) * P], x_in[:, q, k * P:(k + 1) * P], ident[:])
                ins.then_inc(x_turned, 1)

            def gate_at(q, h, gate):
                col = (0, 1, 3, 2)[gate] * HID + h * P
                to = ifg_ps[q][h][:, gate] if gate < 3 else o_ps[q][:, h]
                return to, slice(col, col + P)

            def gates_from_x(q, piece):
                h, rest = divmod(piece, GATES * KC)
                gate, k = divmod(rest, KC)
                to, cols = gate_at(q, h, gate)
                nc.tensor.matmul(to.rearrange("p t s -> p (t s)"), wx_sb[:, k, cols],
                                 XT[:, q, k].rearrange("p t s -> p (t s)"),
                                 start=(k == 0 and (gate == 0 or (gate, h) == (3, 0))), stop=True,
                                 skip_group_check=True)

            def gates_from_bias(q, piece):
                h, gate = divmod(piece, GATES)
                to, cols = gate_at(q, h, gate)
                nc.tensor.matmul(to.rearrange("p t s -> p (t s)"), bias_parts[:, cols], ones_col[:],
                                 start=False, stop=True, skip_group_check=True)

            def l1_product(k, half):
                cols = slice(half * P, (half + 1) * P)
                nc.tensor.matmul(y_ps[:, cols], Z[:, k], w1_sb[:, k, cols], start=(k == 0), stop=(k == KC - 1))

            def l1_turn():
                for k in range(KC):
                    ins = nc.tensor.transpose(r_ps[:, k * P:(k + 1) * P], R[:, k], ident[:])
                ins.then_inc(l1_ready, 1)

            XP = KC * GATES * KC

            def side(n, q, s, first=False, ahead=2):
                if ahead >= 1:
                    if s == 0:
                        pe.wait_ge(XT_ready, n + 2)
                    gates_from_x(1 - q, s)
                    if s >= BT // 2:
                        gates_from_bias(1 - q, s - BT // 2)
                if ahead >= 2 and s == 11:
                    if not first:
                        pe.wait_ge(l1_copied, n)
                    turn_x(n + 2, q)
                if not first:
                    if s == L0:
                        pe.wait_ge(Z_ready, n)
                    if L0 <= s < L0 + 4:
                        l1_product((s - L0) % 2, (s - L0) // 2)
                    if s == L0 + 4:
                        l1_turn()

            def recurrence(n, q, s):
                t = n * BT + s
                window = slice(s - s % WIN, s - s % WIN + WIN)

                def products(k, h, part, w, gates=range(3)):
                    for gate in gates:
                        to, cols = gate_at(q, h, gate)
                        ins = nc.tensor.matmul(to[:, window, :], w[:, k, cols], part[k][:, s % WIN],
                                               start=False, stop=True, skip_group_check=True)
                    return ins

                def hi_products(k, h):
                    products(k, h, H_hi, wh_hi)
                    products(k, h, H_hi, wh_lo)

                pe.wait_ge(hi_made[0], t)
                hi_products(0, 0)
                pe.wait_ge(tg_ready[1], t)
                hi_products(0, 1)
                pe.wait_ge(hi_made[1], t)
                hi_products(1, 0)
                pe.wait_ge(lo_made[0], t)
                products(0, 0, H_lo, wh_hi)
                pe.wait_ge(lo_made[1], t)
                products(1, 0, H_lo, wh_hi).then_inc(gates_ready[0], 1)
                products(0, 1, H_lo, wh_hi)
                hi_products(1, 1)
                products(1, 1, H_lo, wh_hi).then_inc(gates_ready[1], 1)
                for k in range(KC):
                    for part, w in ((H_hi, wh_hi), (H_hi, wh_lo), (H_lo, wh_hi)):
                        for h in HALVES:
                            ins = products(k, h, part, w, [3])
                ins.then_inc(o_summed, 1)

            def steps(n, q, **edge):
                for s in range(BT):
                    if edge.get("first") and s == 0:
                        first_step()
                    else:
                        recurrence(n, q, s)
                    side(n, q, s, **edge)

            def first_step():
                pe.wait_ge(wh_scaled, 1)
                pe.wait_ge(h0_ready, 1)
                def products(h, gate):
                    to, cols = gate_at(0, h, gate)
                    for k in range(KC):
                        ins = nc.tensor.matmul(to[:, 0, :], wh_sb[:, k, cols], h0T[:, k, :],
                                               start=False, stop=True, skip_group_check=True)
                    return ins

                for h in HALVES:
                    for gate in range(3):
                        ins = products(h, gate)
                    ins.then_inc(gates_ready[h], 1)
                products(0, 3)
                products(1, 3).then_inc(o_summed, 1)
                pe.wait_ge(split_ready, 1)

            pe.wait_ge(ident_ready, 1)
            pe.wait_ge(cond_loaded, 16)
            for k in range(KC):
                ins = nc.tensor.transpose(y_ps[:, k * N:(k + 1) * N], cond_sb[:, k * P:(k + 1) * P], ident[0:N, 0:N])
            ins.then_inc(condT_ready, 1)
            turn_x(0, 0)
            pe.wait_ge(XT_ready, 1)
            turn_x(1, 1)
            pe.wait_ge(norm_in, 3)
            for k in range(KC):
                ins = nc.tensor.matmul(y_ps[:, 0:D], ys_sq_rep[:, k].rearrange("p t s -> p (t s)"), w1_sq[:, k, :],
                                       start=(k == 0), stop=(k == KC - 1))
            ins.then_inc(norm_sums, 1)
            pe.wait_ge(wx_scaled, 1)
            pe.wait_ge(bias_ready, 3)
            pe.wait_ge(ones_set, 2)
            for piece in range(XP):
                gates_from_x(0, piece)
            for piece in range(KC * GATES):
                gates_from_bias(0, piece)
            steps(0, 0, first=True)
            steps(1, 1)
            with pe.Fori(1, NB // 2 - 1) as j:
                steps(2 * j, 0)
                steps(2 * j + 1, 1)
            steps(NB - 2, 0, ahead=1)
            steps(NB - 1, 1, ahead=0)
            pe.wait_ge(Z_ready, NB)
            pe.wait_ge(l1_copied, NB - 1)
            for half in range(2):
                for k in range(KC):
                    l1_product(k, half)
            l1_turn()


_INS = ['x', 'cond_1024', 'L0_cond_Wx', 'L0_cond_Wh', 'L0_cond_b', 'L1_cond_weight']
_OUTS = [((8, 256, 256), 'float32')]


def kernel(**inputs):
    import numpy as _np
    import concourse.bacc as _bacc
    from concourse import mybir as _mybir
    from concourse.bass_utils import run_bass_kernel_spmd as _run

    nc = _bacc.Bacc("TRN2", target_bir_lowering=False, num_devices=1)
    arrays, args = {}, []
    for name in _INS:
        a = _np.ascontiguousarray(inputs[name])
        arrays[f"in_{name}_dram"] = a
        args.append(nc.dram_tensor(f"in_{name}_dram", a.shape, _mybir.dt.from_np(a.dtype), kind="ExternalInput").ap())
    for i, (shape, dtype) in enumerate(_OUTS):
        dt = _mybir.dt.from_np(_np.dtype(dtype))
        args.append(nc.dram_tensor(f"out_{i}_dram", shape, dt, kind="ExternalOutput").ap())
    lstm_modulated_residual(nc, *args)
    r = _run(nc, [arrays], core_ids=[0])
    got = tuple(r.results[0][f"out_{i}_dram"] for i in range(len(_OUTS)))
    return got[0]
```

```python
import concourse.bass as bass
from concourse import mybir
from contextlib import ExitStack

F32 = mybir.dt.float32
F16 = mybir.dt.float16
BF16 = mybir.dt.bfloat16
I32 = mybir.dt.int32
ALU = mybir.AluOpType
ACT = mybir.ActivationFunctionType
AX = mybir.AxisListType

P = 128
BT = 16
GATES = 4
EPS = 1e-8
WIN = 4
L0 = 2
LATE = 12
NEWTON = 4
WARM_UPS = (7, 1)


def lstm_modulated_residual(
    nc: bass.Bass,
    x: bass.AP,
    cond: bass.AP,
    Wx: bass.AP,
    Wh: bass.AP,
    b: bass.AP,
    W1: bass.AP,
    out: bass.AP,
):
    N, T, D = x.shape
    HID = D
    KC = D // P
    NB = T // BT
    G4 = GATES * HID
    assert N * BT == P and D == 2 * P and NB % 2 == 0 and NB >= 6
    HALVES = range(KC)
    IFO = 3 * HID

    ctx = ExitStack()
    with ctx:
        def sb(name, shape, dt=F32):
            return ctx.enter_context(nc.sbuf_tensor(name, shape, dt))

        def pb(name, shape, dt=F32):
            return ctx.enter_context(nc.psum_tensor(name, shape, dt))

        def sem(name):
            return ctx.enter_context(nc.semaphore(name))

        wx_sb = sb("wx_sb", [P, KC, G4])
        wh_sb = sb("wh_sb", [P, KC, G4])
        wh_hi = sb("wh_hi", [P, KC, G4], F16)
        wh_lo = sb("wh_lo", [P, KC, G4], F16)
        w1_sb = sb("w1_sb", [P, KC, D])
        w1_sq = sb("w1_sq", [P, KC, D])
        QUAD = 32
        ROWS = GATES * KC
        bias_rows = sb("bias_rows", [3 * QUAD, P])
        bias_rest = sb("bias_rest", [3 * QUAD, P])
        bias_parts = sb("bias_parts", [3 * QUAD, P], BF16)
        bias_sel = sb("bias_sel", [3 * QUAD, ROWS, P], BF16)
        warm = sb("warm", [P, 512], BF16)
        ident = sb("ident", [P, P])
        row_max = sb("row_max", [P, KC])
        all_max = sb("all_max", [P, KC])
        top = sb("top", [P, 1])
        max_pow2 = sb("max_pow2", [P, 1])
        scale_w = sb("scale_w", [P, 1])
        scale_ifo = sb("scale_ifo", [P, 1])
        scale_g = sb("scale_g", [P, 1])
        unscale = sb("unscale", [P, 1])
        cond_sb = sb("cond_sb", [N, D])
        h0T = sb("h0T", [P, 2, KC, BT, N])
        first_gates = sb("first_gates", [P, KC, GATES, N])
        h0_gates = sb("h0_gates", [P, KC, GATES, N])
        ys = sb("ys", [P, KC, N])
        ys_sq = sb("ys_sq", [P, KC, N])
        ys_rep = sb("ys_rep", [P, KC, BT, N])
        ys_sq_rep = sb("ys_sq_rep", [P, KC, BT, N])
        sq_sum = sb("sq_sum", [P, D])
        half_sum = sb("half_sum", [P, D])
        demod = sb("demod", [P, D])
        demod_sq = sb("demod_sq", [P, D])
        x_in = sb("x_in", [P, 2, D])
        XT = sb("XT", [P, 2, KC, BT, N])
        H_all = sb("H_all", [P, 2, KC, BT, N])
        XR = sb("XR", [P, KC, P])
        R = sb("R", [P, KC, P])
        Z = sb("Z", [P, KC, P])
        y_sb = sb("y_sb", [P, D])
        r_sb = sb("r_sb", [P, D])
        yd_sb = sb("yd_sb", [P, D])
        o_sb = sb("o_sb", [P, 2, D])
        tg = [[sb(f"tg{q}{h}", [P, 4, N]) for h in HALVES] for q in range(2)]
        to = [sb(f"to{q}", [P, KC, N]) for q in range(2)]
        uv = [[sb(f"uv{q}{h}", [P, 2, N]) for h in HALVES] for q in range(2)]
        tc = [[sb(f"tc{q}{h}", [P, N]) for h in HALVES] for q in range(2)]
        H_hi = [sb(f"H_hi{h}", [P, WIN, WIN, N], F16) for h in HALVES]
        H_lo = [sb(f"H_lo{h}", [P, WIN, WIN, N], F16) for h in HALVES]

        ifg_ps = [[pb(f"ifg_ps{q}{h}", [P, 4, BT, N]) for h in HALVES] for q in range(2)]
        o_ps = [pb(f"o_ps{q}", [P, 2 * KC, BT, N]) for q in range(2)]
        turn_ps = pb("turn_ps", [P, 512])
        xT_ps = turn_ps[:, 0:KC * P]
        r_ps = turn_ps[:, KC * P:2 * KC * P]
        y_ps = pb("y_ps", [P, 512])
        condT_ps = y_ps[:, 0:KC * N].rearrange("p (k s) -> p k s", k=KC)
        h0_ps = ifg_ps[1]

        x_loaded = [sem(f"x_loaded{q}") for q in range(2)]
        wx_loaded = [sem(f"wx_loaded{k}") for k in range(KC)]
        wh_loaded = [sem(f"wh_loaded{k}") for k in range(KC)]
        b_loaded = sem("b_loaded")
        w1_loaded = sem("w1_loaded")
        cond_loaded = sem("cond_loaded")
        out_stored = [sem(f"out_stored{q}") for q in range(2)]
        warm_set = sem("warm_set")
        bias_cleared = sem("bias_cleared")
        sel_zero = sem("sel_zero")
        sel_ready = sem("sel_ready")
        ident_zero = sem("ident_zero")
        ident_ready = sem("ident_ready")
        prep = sem("prep")
        max_ready = sem("max_ready")
        allmax_ready = sem("allmax_ready")
        condT_ready = sem("condT_ready")
        ys_ready = sem("ys_ready")
        h0_cleared = sem("h0_cleared")
        h0_ready = sem("h0_ready")
        h0_summed = sem("h0_summed")
        h0_scaled = sem("h0_scaled")
        first_summed = sem("first_summed")
        wx_scaled = [sem(f"wx_scaled{k}") for k in range(KC)]
        bias_ready = sem("bias_ready")
        scale_ready = sem("scale_ready")
        hi_ready = sem("hi_ready")
        g_hi_ready = sem("g_hi_ready")
        split_ready = sem("split_ready")
        c0_ready = sem("c0_ready")
        ysq_ready = sem("ysq_ready")
        norm_in = sem("norm_in")
        norm_sums = sem("norm_sums")
        sums_ready = sem("sums_ready")
        bits_ready = sem("bits_ready")
        pool_prep = sem("pool_prep")
        gates_ready = [sem(f"gates_ready{h}") for h in HALVES]
        tg_ready = [sem(f"tg_ready{h}") for h in HALVES]
        o_summed = sem("o_summed")
        uv_ready = [sem(f"uv_ready{h}") for h in HALVES]
        c_ready = [sem(f"c_ready{h}") for h in HALVES]
        tc_ready = [sem(f"tc_ready{h}") for h in HALVES]
        hi_made = [sem(f"hi_made{h}") for h in HALVES]
        full_made = [sem(f"full_made{h}") for h in HALVES]
        lo_made = [sem(f"lo_made{h}") for h in HALVES]
        x_turned = sem("x_turned")
        XT_ready = sem("XT_ready")
        XR_ready = sem("XR_ready")
        R_ready = sem("R_ready")
        Z_ready = sem("Z_ready")
        l1_ready = sem("l1_ready")
        l1_copied = sem("l1_copied")
        yd_ready = sem("yd_ready")
        o_ready = sem("o_ready")
        RZ_early = sem("RZ_early")
        R_late = sem("R_late")
        Z_late = sem("Z_late")
        y_late = sem("y_late")
        yd_late = sem("yd_late")
        o_late = sem("o_late")

        y_late_ps = [y_ps[:, 0:P], ifg_ps[0][0][:, 0].rearrange("p t s -> p (t s)")]

        def by_step(rows):
            return rows[:].rearrange("p k (t s) -> p k t s", s=N)

        x_rows = x.rearrange("s t d -> t s d")
        out_rows = out.rearrange("s t d -> t s d")
        w_view = "(k p) n -> p k n"

        block = ctx.enter_context(nc.Block())

        @block.sync
        def _(sp):
            def load_x(n, q):
                sp.dma_start(x_in[:, q, :], x_rows[bass.ds(n * BT, BT)]).then_inc(x_loaded[q], 16)

            def block_io(n, q, first=False, ahead=2):
                if ahead >= 2:
                    sp.wait_ge(x_turned, n + 1)
                    load_x(n + 2, q)
                if not first:
                    sp.wait_ge(o_ready, n)
                    sp.dma_start(out_rows[bass.ds((n - 1) * BT, BT)], o_sb[:, 1 - q, :]).then_inc(out_stored[1 - q], 16)

            for k in range(KC):
                sp.dma_start(wh_sb[:, k, :], Wh[k * P:(k + 1) * P, :]).then_inc(wh_loaded[k], 16)
            sp.wait_ge(bias_cleared, 1)
            for i in range(3):
                sp.dma_start(bias_rows[QUAD * i:QUAD * i + ROWS, :], b.rearrange("(r n) -> r n", n=P)).then_inc(b_loaded, 16)
            for k in range(KC):
                sp.dma_start(wx_sb[:, k, :], Wx[k * P:(k + 1) * P, :]).then_inc(wx_loaded[k], 16)
            load_x(1, 1)
            block_io(0, 0, first=True)
            block_io(1, 1)
            with sp.Fori(1, NB // 2 - 1) as j:
                block_io(2 * j, 0)
                block_io(2 * j + 1, 1)
            block_io(NB - 2, 0, ahead=1)
            block_io(NB - 1, 1, ahead=0)
            sp.wait_ge(o_late, 2)
            sp.dma_start(out_rows[(NB - 1) * BT:], o_sb[:, 1, :]).then_inc(out_stored[1], 16)
            for q in range(2):
                sp.wait_ge(out_stored[q], 16 * NB // 2)

        @block.scalar
        def _(act):
            act.dma_start(cond_sb[:], cond).then_inc(cond_loaded, 16)
            act.dma_start(x_in[:, 0, :], x_rows[0:BT]).then_inc(x_loaded[0], 16)
            act.dma_start(w1_sb[:], W1.rearrange(w_view, p=P)).then_inc(w1_loaded, 16)

            def copy_xT(n, q, piece):
                w = KC * P // 4
                flat = XT[:, q].rearrange("p k t s -> p (k t s)")
                ins = nc.scalar.mul(flat[:, piece * w:(piece + 1) * w], xT_ps[:, piece * w:(piece + 1) * w], 2.0)
                if piece == 3:
                    ins.then_inc(XT_ready, 1)

            def copy_l1(piece):
                w = D // 4
                at = slice(piece % 4 * w, (piece % 4 + 1) * w)
                if piece < 4:
                    nc.scalar.copy(y_sb[:, at], y_ps[:, at])
                else:
                    ins = nc.scalar.mul(r_sb[:, at], r_ps[:, at], 0.5)
                    if piece == 7:
                        ins.then_inc(l1_copied, 1)

            def side(n, q, s, first=False, ahead=2):
                if not first and 7 <= s < 11:
                    if s == 7:
                        if not isinstance(n, int) or n > 1:
                            act.wait_ge(o_ready, n - 1)
                        act.wait_ge(l1_ready, n)
                    copy_l1(2 * (s - 7))
                    copy_l1(2 * (s - 7) + 1)
                if ahead >= 2 and 12 <= s < 14:
                    if s == 12:
                        act.wait_ge(XR_ready, n + 1)
                        act.wait_ge(x_turned, n + 3)
                    copy_xT(n + 2, q, 2 * (s - 12))
                    copy_xT(n + 2, q, 2 * (s - 12) + 1)

            def steps(n, q, **edge):
                for s in range(BT):
                    r = s % 2
                    very_first = edge.get("first") and s == 0
                    for h in HALVES:
                        act.wait_ge(gates_ready[h], n * BT + s + 1)
                        gates = first_gates[:, h, 0:3] if very_first else ifg_ps[q][h][:, 0:3, s, :]
                        nc.scalar.activation(tg[r][h][:, 0:3, :], gates, ACT.Tanh,
                                             scale=unscale_reg).then_inc(tg_ready[h], 1)
                    act.wait_ge(o_summed, n * BT + s + 1)
                    gates = first_gates[:, :, 3] if very_first else o_ps[q][:, 0:KC, s, :]
                    nc.scalar.activation(to[r][:], gates, ACT.Tanh, scale=unscale_reg)
                    for h in HALVES:
                        act.wait_ge(c_ready[h], n * BT + s + 1)
                        nc.scalar.activation(tc[r][h][:], tg[1 - r][h][:, 3, :], ACT.Tanh,
                                             scale=0.5).then_inc(tc_ready[h], 1)
                    side(n, q, s, **edge)

            def first_x(n):
                act.wait_ge(x_turned, n + 1)
                for piece in range(4):
                    copy_xT(n, n, piece)

            first_x(0)
            act.wait_ge(wx_loaded[0], 16)
            act.wait_ge(scale_ready, 1)
            nc.scalar.mul(wx_sb[:, 0, 0:IFO], wx_sb[:, 0, 0:IFO], scale_ifo[:]).then_inc(wx_scaled[0], 1)
            nc.scalar.mul(wx_sb[:, 0, IFO:G4], wx_sb[:, 0, IFO:G4], scale_g[:]).then_inc(wx_scaled[0], 1)
            nc.scalar.mul(wh_hi[:, :, IFO:G4], wh_sb[:, :, IFO:G4], scale_g[:]).then_inc(g_hi_ready, 1)
            first_x(1)
            unscale_reg = ctx.enter_context(act.register("unscale_reg"))
            nc.scalar.reg_load(unscale_reg, unscale[0:1, 0:1].bitcast(I32))
            steps(0, 0, first=True)
            steps(1, 1)
            with act.Fori(1, NB // 2 - 1) as j:
                steps(2 * j, 0)
                steps(2 * j + 1, 1)
            steps(NB - 2, 0, ahead=1)
            steps(NB - 1, 1, ahead=0)

        @block.vector
        def _(dve):
            count = [0]

            def done(ins):
                count[0] += 1
                ins.then_inc(prep, 1)
                dve.wait_ge(prep, count[0])

            nc.vector.memset(warm[:], 0.0).then_inc(warm_set, 1)
            nc.vector.memset(bias_rows[:], 0.0).then_inc(bias_cleared, 1)
            nc.vector.memset(h0T[:].rearrange("p v k t s -> p (v k t s)"), 0.0).then_inc(h0_cleared, 1)
            for h in HALVES:
                nc.vector.memset(tg[0][h][:, 3, :], 0.0).then_inc(c0_ready, 1)
                for part in (H_hi, H_lo):
                    nc.vector.memset(part[h][:].rearrange("p w t s -> p (w t s)").bitcast(I32), 0).then_inc(c0_ready, 1)
            dve.wait_ge(condT_ready, 1)
            nc.vector.tensor_scalar(ys[:], condT_ps, float(D) ** -0.5, None, ALU.mult).then_inc(ys_ready, 1)
            dve.wait_ge(h0_cleared, 1)
            for v, factor in enumerate((0.5, 1.0)):
                nc.vector.tensor_scalar(h0T[:, v, :, 0, :], condT_ps, factor, None, ALU.mult).then_inc(h0_ready, 1)
            for k in range(KC):
                dve.wait_ge(wh_loaded[k], 16)
                nc.vector.tensor_reduce(row_max[:, k:k + 1], wh_sb[:, k, :], AX.X, ALU.max,
                                        apply_absolute_value=True).then_inc(max_ready, 1)
            dve.wait_ge(allmax_ready, 1)
            done(nc.vector.tensor_reduce(top[:], all_max[:], AX.X, ALU.max))
            done(nc.vector.tensor_scalar(max_pow2[:].bitcast(I32), top[:].bitcast(I32), 0x7F800000, None, ALU.bitwise_and))
            done(nc.vector.tensor_scalar(unscale[:], max_pow2[:], 2.0 ** -30, 2.0 ** -14, ALU.max, ALU.mult))
            done(nc.vector.reciprocal(scale_w[:], unscale[:]))
            nc.vector.tensor_scalar(scale_ifo[:], scale_w[:], 0.25, None, ALU.mult)
            nc.vector.tensor_scalar(scale_g[:], scale_w[:], 0.5, None, ALU.mult).then_inc(scale_ready, 1)
            dve.wait_ge(scale_ready, 1)
            nc.vector.tensor_scalar(wh_hi[:, :, 0:IFO], wh_sb[:, :, 0:IFO], scale_ifo[:], None, ALU.mult).then_inc(hi_ready, 1)
            dve.wait_ge(wx_loaded[1], 16)
            nc.vector.tensor_scalar(wx_sb[:, 1, 0:IFO], wx_sb[:, 1, 0:IFO], scale_ifo[:], None, ALU.mult).then_inc(wx_scaled[1], 1)
            nc.vector.tensor_scalar(wx_sb[:, 1, IFO:G4], wx_sb[:, 1, IFO:G4], scale_g[:], None, ALU.mult).then_inc(wx_scaled[1], 1)
            dve.wait_ge(h0_summed, 1)
            for h in HALVES:
                nc.vector.tensor_scalar(h0_gates[:, h], h0_ps[h][:, :, 0, :], scale_w[:], None, ALU.mult).then_inc(h0_scaled, 1)
            dve.wait_ge(hi_ready, 1)
            dve.wait_ge(g_hi_ready, 1)
            for cols, scale in ((slice(0, IFO), scale_ifo), (slice(IFO, G4), scale_g)):
                nc.vector.scalar_tensor_tensor(out=wh_lo[:, :, cols], in0=wh_sb[:, :, cols], scalar=scale[:],
                                               in1=wh_hi[:, :, cols], op0=ALU.mult,
                                               op1=ALU.subtract).then_inc(split_ready, 1)

            dve.wait_ge(h0_scaled, 2)
            for h in HALVES:
                dve.wait_ge(first_summed, h + 1)
                nc.vector.tensor_tensor(first_gates[:, h, 0:3], h0_gates[:, h, 0:3], ifg_ps[0][h][:, 0:3, 0, :],
                                        ALU.add).then_inc(gates_ready[h], 1)

            def cell(n, h, s):
                r = s % 2
                dve.wait_ge(tg_ready[h], n * BT + s + 1)
                nc.vector.scalar_tensor_tensor(out=uv[r][h][:], in0=tg[r][h][:, 0:2, :], scalar=1.0,
                                               in1=tg[r][h][:, 2:4, :], op0=ALU.add,
                                               op1=ALU.mult).then_inc(uv_ready[h], 1)
                dve.wait_ge(uv_ready[h], n * BT + s + 1)
                nc.vector.scalar_tensor_tensor(out=tg[1 - r][h][:, 3, :], in0=uv[r][h][:, 1, :], scalar=0.5,
                                               in1=uv[r][h][:, 0, :], op0=ALU.mult,
                                               op1=ALU.add).then_inc(c_ready[h], 1)

            def hidden_hi(n, h, s):
                r = s % 2
                dve.wait_ge(tc_ready[h], n * BT + s + 1)
                w = (s + 1) % WIN
                nc.vector.scalar_tensor_tensor(out=H_hi[h][:, w, w, :], in0=to[r][:, h, :], scalar=1.0, in1=tc[r][h][:],
                                               op0=ALU.add, op1=ALU.mult).then_inc(hi_made[h], 1)

            def hidden(n, q, h, s):
                r = s % 2
                nc.vector.scalar_tensor_tensor(out=H_all[:, q, h, s, :], in0=to[r][:, h, :], scalar=1.0, in1=tc[r][h][:],
                                               op0=ALU.add, op1=ALU.mult).then_inc(full_made[h], 1)

            def hidden_lo(n, q, h, s):
                w = (s + 1) % WIN
                dve.wait_ge(full_made[h], n * BT + s + 1)
                nc.vector.tensor_tensor(H_lo[h][:, w, w, :], H_all[:, q, h, s, :], H_hi[h][:, w, w, :],
                                        ALU.subtract).then_inc(lo_made[h], 1)

            def steps(n, q, first=False):
                for s in range(BT):
                    for h in HALVES:
                        cell(n, h, s)
                        if first and s == 0 and h == 0:
                            dve.wait_ge(first_summed, 3)
                            nc.vector.tensor_tensor(first_gates[:, :, 3], h0_gates[:, :, 3], o_ps[0][:, 0:KC, 0, :],
                                                    ALU.add).then_inc(o_summed, 1)
                    if isinstance(n, int) and n == NB - 1 and s == BT - 1:
                        dve.wait_ge(RZ_early, 2)
                        for h in HALVES:
                            dve.wait_ge(tc_ready[h], NB * BT)
                            hidden(n, q, h, s)
                        continue
                    hidden_hi(n, 0, s)
                    hidden(n, q, 0, s)
                    hidden_hi(n, 1, s)
                    hidden(n, q, 1, s)
                    hidden_lo(n, q, 0, s)
                    hidden_lo(n, q, 1, s)
                    if first and s == 5:
                        dve.wait_ge(norm_sums, 1)
                        nc.vector.tensor_scalar(sq_sum[:], y_ps[:, 0:D], EPS, None, ALU.add).then_inc(sums_ready, 1)
                    if first and s == 6:
                        dve.wait_ge(sums_ready, 1)
                        nc.vector.tensor_scalar(demod[:].bitcast(I32), sq_sum[:].bitcast(I32), 1, None,
                                                ALU.logical_shift_right).then_inc(bits_ready, 1)
                if not isinstance(n, int) or 0 < n < NB - 1:
                    dve.wait_ge(R_ready, n)

            dve.wait_ge(c0_ready, 3 * KC)
            steps(0, 0, first=True)
            steps(1, 1)
            with dve.Fori(1, NB // 2 - 1) as j:
                steps(2 * j, 0)
                steps(2 * j + 1, 1)
            steps(NB - 2, 0)
            steps(NB - 1, 1)

            for h in HALVES:
                dve.wait_ge(full_made[h], NB * BT)
            late = slice(LATE, BT)
            nc.vector.tensor_tensor(by_step(R)[:, :, late], H_all[:, 1, :, late], by_step(XR)[:, :, late],
                                    ALU.add).then_inc(R_late, 1)
            dve.wait_ge(R_late, 1)
            nc.vector.tensor_tensor(by_step(Z)[:, :, late], by_step(R)[:, :, late], ys_rep[:, :, late],
                                    ALU.mult).then_inc(Z_late, 1)
            dve.wait_ge(o_ready, NB - 1)
            dve.wait_ge(out_stored[1], 8 * (NB - 2))
            columns = [slice(half * P, (half + 1) * P) for half in range(2)]
            for half, cols in enumerate(columns):
                dve.wait_ge(y_late, half + 1)
                nc.vector.tensor_tensor(yd_sb[:, cols], y_late_ps[half], demod[:, cols], ALU.mult).then_inc(yd_late, 1)
            for half, cols in enumerate(columns):
                dve.wait_ge(yd_late, half + 1)
                nc.vector.scalar_tensor_tensor(out=o_sb[:, 1, cols], in0=r_ps[:, cols], scalar=0.5, in1=yd_sb[:, cols],
                                               op0=ALU.mult, op1=ALU.add).then_inc(o_late, 1)

        @block.gpsimd
        def _(pool):
            nc.gpsimd.memset(ident[:], 0.0).then_inc(ident_zero, 1)
            pool.wait_ge(ident_zero, 1)
            nc.gpsimd.affine_select(out=ident[:], in_=ident[:], compare_op=ALU.not_equal, fill=1.0, base=0,
                                    pattern=[[-1, P]], channel_multiplier=1).then_inc(ident_ready, 1)
            nc.gpsimd.memset(bias_sel[:], 0.0).then_inc(sel_zero, 1)
            pool.wait_ge(sel_zero, 1)
            for g, (rows, factor) in enumerate((((0, 3 * KC), 0.5), ((3 * KC, ROWS), 1.0))):
                for i in range(3):
                    if i > 0:
                        pool.wait_ge(sel_ready, 3 * g + i)
                    part = bias_sel[:, rows[0]:rows[1], :]
                    nc.gpsimd.affine_select(out=part, in_=part, compare_op=ALU.not_equal, fill=factor,
                                            base=-QUAD * i - rows[0], pattern=[[-1, rows[1] - rows[0]], [0, P]],
                                            channel_multiplier=1).then_inc(sel_ready, 1)
            pool.wait_ge(max_ready, KC)
            nc.gpsimd.partition_all_reduce(all_max[:], row_max[:], P, bass.bass_isa.ReduceOp.max).then_inc(allmax_ready, 1)
            count = [0]

            def done(ins):
                count[0] += 1
                ins.then_inc(pool_prep, 1)
                pool.wait_ge(pool_prep, count[0])

            pool.wait_ge(b_loaded, 48)
            done(nc.gpsimd.tensor_copy(bias_parts[:], bias_rows[:]))
            done(nc.gpsimd.tensor_tensor(bias_rest[:], bias_rows[:], bias_parts[:], ALU.subtract))
            second, third = slice(QUAD, 2 * QUAD), slice(2 * QUAD, 3 * QUAD)
            nc.gpsimd.tensor_copy(bias_parts[second, :], bias_rest[second, :])
            done(nc.gpsimd.tensor_copy(bias_parts[third, :], bias_rest[third, :]))
            done(nc.gpsimd.tensor_tensor(bias_rest[third, :], bias_rest[third, :], bias_parts[third, :], ALU.subtract))
            done(nc.gpsimd.tensor_copy(bias_parts[third, :], bias_rest[third, :]))
            pool.wait_ge(scale_ready, 1)
            nc.gpsimd.tensor_scalar(bias_parts[:], bias_parts[:], scale_w[0:3 * QUAD, :], None, ALU.mult).then_inc(bias_ready, 1)
            pool.wait_ge(ys_ready, 1)
            done(nc.gpsimd.tensor_tensor(ys_sq[:], ys[:], ys[:], ALU.mult))
            for k in range(KC):
                nc.gpsimd.tensor_copy(ys_sq_rep[:, k], ys_sq[:, k:k + 1, :].to_broadcast([P, BT, N])).then_inc(norm_in, 1)
            pool.wait_ge(w1_loaded, 16)
            nc.gpsimd.tensor_tensor(w1_sq[:], w1_sb[:], w1_sb[:], ALU.mult).then_inc(norm_in, 1)
            for k in range(KC):
                nc.gpsimd.tensor_scalar(ys_rep[:, k], ys[:, k:k + 1, :].to_broadcast([P, BT, N]), 0.5, None,
                                        ALU.mult).then_inc(ysq_ready, 1)

            def modulate(n, q):
                pool.wait_ge(XT_ready, n + 2)
                for h in HALVES:
                    pool.wait_ge(full_made[h], (n + 1) * BT)
                if not isinstance(n, int) or n > 0:
                    pool.wait_ge(l1_ready, n)
                flat = "p k t s -> p (k t s)"
                Rf = R[:].rearrange("p k m -> p (k m)")
                pool.wait_ge(XR_ready, n + 1)
                nc.gpsimd.tensor_tensor(Rf, H_all[:, q].rearrange(flat), XR[:].rearrange("p k m -> p (k m)"),
                                        ALU.add).then_inc(R_ready, 1)
                pool.wait_ge(R_ready, n + 1)
                nc.gpsimd.tensor_tensor(Z[:].rearrange("p k m -> p (k m)"), Rf, ys_rep[:].rearrange(flat),
                                        ALU.mult).then_inc(Z_ready, 1)
                keep_x(1 - q)

            def keep_x(q):
                nc.gpsimd.tensor_copy(XR[:].rearrange("p k m -> p (k m)"),
                                      XT[:, q].rearrange("p k t s -> p (k t s)")).then_inc(XR_ready, 1)

            def finish(n, q):
                pool.wait_ge(l1_copied, n + 1)
                nc.gpsimd.tensor_tensor(yd_sb[:], y_sb[:], demod[:], ALU.mult).then_inc(yd_ready, 1)
                pool.wait_ge(yd_ready, n + 1)
                if not isinstance(n, int) or n > 1:
                    pool.wait_ge(out_stored[q], 8 * (n - q))
                nc.gpsimd.tensor_tensor(o_sb[:, q, :], yd_sb[:], r_sb[:], ALU.add).then_inc(o_ready, 1)

            pool.wait_ge(XT_ready, 1)
            keep_x(0)
            pool.wait_ge(ysq_ready, 2)
            pool.wait_ge(sums_ready, 1)
            nc.gpsimd.tensor_scalar(half_sum[:], sq_sum[:], 0.5, None, ALU.mult)
            pool.wait_ge(bits_ready, 1)
            done(nc.gpsimd.tensor_scalar(demod[:].bitcast(I32), demod[:].bitcast(I32), -1, 0x5F3759DF, ALU.mult, ALU.add))
            for _ in range(NEWTON):
                done(nc.gpsimd.tensor_tensor(demod_sq[:], demod[:], demod[:], ALU.mult))
                done(nc.gpsimd.tensor_tensor(demod_sq[:], demod_sq[:], half_sum[:], ALU.mult))
                done(nc.gpsimd.tensor_scalar(demod_sq[:], demod_sq[:], -1.0, 1.5, ALU.mult, ALU.add))
                done(nc.gpsimd.tensor_tensor(demod[:], demod[:], demod_sq[:], ALU.mult))
            for n in range(2):
                modulate(n, n)
                finish(n, n)
            with pool.Fori(1, NB // 2 - 1) as j:
                for q in range(2):
                    modulate(2 * j + q, q)
                    finish(2 * j + q, q)
            modulate(NB - 2, 0)
            finish(NB - 2, 0)
            early = slice(0, LATE)
            for h in HALVES:
                pool.wait_ge(full_made[h], (NB - 1) * BT + LATE)
            pool.wait_ge(l1_ready, NB - 1)
            pool.wait_ge(XR_ready, NB)
            nc.gpsimd.tensor_tensor(by_step(R)[:, :, early], H_all[:, 1, :, early], by_step(XR)[:, :, early],
                                    ALU.add).then_inc(RZ_early, 1)
            pool.wait_ge(RZ_early, 1)
            nc.gpsimd.tensor_tensor(by_step(Z)[:, :, early], by_step(R)[:, :, early], ys_rep[:, :, early],
                                    ALU.mult).then_inc(RZ_early, 1)

        @block.tensor
        def _(pe):
            def turn_x(n, q):
                pe.wait_ge(x_loaded[q], 8 * (n - q) + 16)
                for k in range(KC):
                    ins = nc.tensor.transpose(xT_ps[:, k * P:(k + 1) * P], x_in[:, q, k * P:(k + 1) * P], ident[:])
                ins.then_inc(x_turned, 1)

            def gate_at(q, h, gate):
                col = (0, 1, 3, 2)[gate] * HID + h * P
                to = ifg_ps[q][h][:, gate] if gate < 3 else o_ps[q][:, h]
                return to, slice(col, col + P)

            def opens_bank(h, gate):
                return gate == 0 or (gate == 3 and h == 0)

            def gates_from_x(q, piece):
                h, rest = divmod(piece, GATES * KC)
                gate, k = divmod(rest, KC)
                to, cols = gate_at(q, h, gate)
                return nc.tensor.matmul(to.rearrange("p t s -> p (t s)"), wx_sb[:, k, cols],
                                        XT[:, q, k].rearrange("p t s -> p (t s)"),
                                        start=(k == 0 and opens_bank(h, gate)), stop=True, skip_group_check=True)

            def gates_from_bias(q, piece):
                h, gate = divmod(piece, GATES)
                to, _ = gate_at(q, h, gate)
                row = (0, 1, 3, 2)[gate] * KC + h
                return nc.tensor.matmul(to.rearrange("p t s -> p (t s)"), bias_parts[:], bias_sel[:, row, :],
                                        start=False, stop=True, skip_group_check=True)

            def l1_product(k, half):
                cols = slice(half * P, (half + 1) * P)
                nc.tensor.matmul(y_ps[:, cols], Z[:, k], w1_sb[:, k, cols], start=(k == 0), stop=(k == KC - 1))

            def l1_turn():
                for k in range(KC):
                    ins = nc.tensor.transpose(r_ps[:, k * P:(k + 1) * P], R[:, k], ident[:])
                ins.then_inc(l1_ready, 1)

            def side(n, q, s, first=False, ahead=2):
                if first and 1 <= s < 5:
                    half, k = divmod(s - 1, 2)
                    cols = slice(half * P, (half + 1) * P)
                    if s == 1:
                        pe.wait_ge(norm_in, 3)
                    ins = nc.tensor.matmul(y_ps[:, cols], ys_sq_rep[:, k].rearrange("p t s -> p (t s)"),
                                           w1_sq[:, k, cols], start=(k == 0), stop=(k == KC - 1))
                    if s == 4:
                        ins.then_inc(norm_sums, 1)
                if ahead == 0:
                    warm_up(1, o_ps[0])
                if ahead >= 1:
                    if s == 0:
                        pe.wait_ge(XT_ready, n + 2)
                    gates_from_x(1 - q, s)
                    if s >= BT // 2:
                        gates_from_bias(1 - q, s - BT // 2)
                if ahead >= 2 and s == 11:
                    if not first:
                        pe.wait_ge(l1_copied, n)
                    turn_x(n + 2, q)
                if not first:
                    if s == L0:
                        pe.wait_ge(Z_ready, n)
                    if L0 <= s < L0 + 4:
                        l1_product((s - L0) % 2, (s - L0) // 2)
                    if s == L0 + 4:
                        l1_turn()

            def recurrence(n, q, s):
                t = n * BT + s
                window = slice(s - s % WIN, s - s % WIN + WIN)

                def products(k, h, part, w, gates=range(3)):
                    for gate in gates:
                        to, cols = gate_at(q, h, gate)
                        ins = nc.tensor.matmul(to[:, window, :], w[:, k, cols], part[k][:, s % WIN],
                                               start=False, stop=True, skip_group_check=True)
                    return ins

                def hi_products(k, h):
                    products(k, h, H_hi, wh_hi)
                    products(k, h, H_hi, wh_lo)

                pe.wait_ge(hi_made[0], t)
                hi_products(0, 0)
                pe.wait_ge(tg_ready[1], t)
                hi_products(0, 1)
                pe.wait_ge(hi_made[1], t)
                hi_products(1, 0)
                pe.wait_ge(lo_made[0], t)
                products(0, 0, H_lo, wh_hi)
                products(0, 1, H_lo, wh_hi, [0])
                pe.wait_ge(lo_made[1], t)
                products(1, 0, H_lo, wh_hi).then_inc(gates_ready[0], 1)
                products(0, 1, H_lo, wh_hi, [1, 2])
                hi_products(1, 1)
                products(1, 1, H_lo, wh_hi).then_inc(gates_ready[1], 1)
                for k in range(KC):
                    for part, w in ((H_hi, wh_hi), (H_hi, wh_lo), (H_lo, wh_hi)):
                        for h in HALVES:
                            ins = products(k, h, part, w, [3])
                ins.then_inc(o_summed, 1)

            def steps(n, q, **edge):
                for s in range(BT):
                    if s == 1 and edge.get("first"):
                        pe.wait_ge(split_ready, 2)
                    if s > 0 or not edge.get("first"):
                        recurrence(n, q, s)
                    side(n, q, s, **edge)

            def from_h0(h, gate, k):
                _, cols = gate_at(0, h, gate)
                return nc.tensor.matmul(h0_ps[h][:, gate].rearrange("p t s -> p (t s)"), wh_sb[:, k, cols],
                                        h0T[:, gate == 2, k].rearrange("p t s -> p (t s)"),
                                        start=(k == 0 and gate == 0), stop=True, skip_group_check=True)

            def warm_up(times, bank):
                for _ in range(times):
                    nc.tensor.matmul(bank[:].rearrange("p a t s -> p (a t s)"), warm[:, 0:P], warm[:], start=True, stop=True)

            pe.wait_ge(warm_set, 1)
            warm_up(WARM_UPS[0], o_ps[1])
            pe.wait_ge(ident_ready, 1)
            pe.wait_ge(cond_loaded, 16)
            for k in range(KC):
                ins = nc.tensor.transpose(y_ps[:, k * N:(k + 1) * N], cond_sb[:, k * P:(k + 1) * P], ident[0:N, 0:N])
            ins.then_inc(condT_ready, 1)
            warm_up(WARM_UPS[1], o_ps[1])
            pe.wait_ge(h0_ready, 2)
            for k in range(KC):
                pe.wait_ge(wh_loaded[k], 16)
                for h in HALVES:
                    for gate in range(GATES):
                        ins = from_h0(h, gate, k)
                    if k == KC - 1 and h == KC - 1:
                        ins.then_inc(h0_summed, 1)
                if k == 0:
                    turn_x(0, 0)
            pe.wait_ge(XT_ready, 1)
            turn_x(1, 1)
            for gate in range(GATES):
                pe.wait_ge(wx_scaled[0], 2 if gate == 2 else 1)
                for h in HALVES:
                    gates_from_x(0, (GATES * h + gate) * KC)
            pe.wait_ge(wx_scaled[1], 2)
            pe.wait_ge(sel_ready, 6)
            pe.wait_ge(bias_ready, 1)
            for gates in ([(0, 0), (0, 1), (0, 2)], [(1, 0), (1, 1), (1, 2)], [(0, 3), (1, 3)]):
                for h, gate in gates:
                    gates_from_x(0, (GATES * h + gate) * KC + 1)
                for h, gate in gates:
                    ins = gates_from_bias(0, GATES * h + gate)
                ins.then_inc(first_summed, 1)
            pe.wait_ge(h0_scaled, 2)
            steps(0, 0, first=True)
            steps(1, 1)
            with pe.Fori(1, NB // 2 - 1) as j:
                steps(2 * j, 0)
                steps(2 * j + 1, 1)
            steps(NB - 2, 0, ahead=1)
            steps(NB - 1, 1, ahead=0)
            warm_up(2, o_ps[0])
            pe.wait_ge(RZ_early, 2)
            pe.wait_ge(l1_copied, NB - 1)
            pe.wait_ge(R_late, 1)
            for k in range(KC):
                nc.tensor.transpose(r_ps[:, k * P:(k + 1) * P], R[:, k], ident[:])
            pe.wait_ge(Z_late, 1)
            for half in range(2):
                for k in range(KC):
                    ins = nc.tensor.matmul(y_late_ps[half], Z[:, k], w1_sb[:, k, half * P:(half + 1) * P],
                                           start=(k == 0), stop=(k == KC - 1))
                ins.then_inc(y_late, 1)


_INS = ['x', 'cond_1024', 'L0_cond_Wx', 'L0_cond_Wh', 'L0_cond_b', 'L1_cond_weight']
_OUTS = [((8, 256, 256), 'float32')]


def kernel(**inputs):
    import numpy as _np
    import concourse.bacc as _bacc
    from concourse import mybir as _mybir
    from concourse.bass_utils import run_bass_kernel_spmd as _run

    nc = _bacc.Bacc("TRN2", target_bir_lowering=False, num_devices=1)
    arrays, args = {}, []
    for name in _INS:
        a = _np.ascontiguousarray(inputs[name])
        arrays[f"in_{name}_dram"] = a
        args.append(nc.dram_tensor(f"in_{name}_dram", a.shape, _mybir.dt.from_np(a.dtype), kind="ExternalInput").ap())
    for i, (shape, dtype) in enumerate(_OUTS):
        dt = _mybir.dt.from_np(_np.dtype(dtype))
        args.append(nc.dram_tensor(f"out_{i}_dram", shape, dt, kind="ExternalOutput").ap())
    lstm_modulated_residual(nc, *args)
    r = _run(nc, [arrays], core_ids=[0])
    got = tuple(r.results[0][f"out_{i}_dram"] for i in range(len(_OUTS)))
    return got[0]
```
